# Optimizing a Trainium2 kernel written in Bass

```python
import numpy as np
import jax
import jax.numpy as jnp

def _softmax(x, axis=-1):
    return jax.nn.softmax(x, axis=axis)

def _gelu(x):
    return jax.nn.gelu(x, approximate=True)

def _silu(x):
    return jax.nn.silu(x)

def _sigmoid(x):
    return jax.nn.sigmoid(x)

def _layernorm(x, axis=-1, eps=1e-05):
    m = jnp.mean(x, axis=axis, keepdims=True)
    v = jnp.var(x, axis=axis, keepdims=True)
    return (x - m) / jnp.sqrt(v + eps)

def _scatter_add(tgt, idx, src, axis=0):
    return tgt.at[idx].add(src)

def _segment_sum(src, seg, n):
    return jax.ops.segment_sum(src, seg, n)
kernel_name = 'mk_gnn_resnorm_d4_gnn_r64_822c5d'

def setup_inputs(seed: int=0):
    np.random.seed(seed)
    _w = jnp.asarray

    def _rec_inputs():
        import jax
        import jax.numpy as jnp
        _gk = jax.random.key(seed)
        x = -0.0005121 + 1.001 * jax.random.normal(jax.random.fold_in(_gk, 1), (100000, 64), jnp.float32)
        src = jax.random.randint(jax.random.fold_in(_gk, 2), (25000,), 0, 100000, jnp.int32)
        dst = jnp.minimum((100000 * jax.random.uniform(jax.random.fold_in(_gk, 3), (25000,)) ** 2.0).astype(jnp.int32), 99999)
        _o = jnp.argsort(dst, stable=True)
        src = src[_o]
        dst = dst[_o]
        edge_attr_32 = 0.000216709 + 1.00012 * jax.random.normal(jax.random.fold_in(_gk, 12), (25000, 32), jnp.float32)
        return (x, src, dst, edge_attr_32)
    x, src, dst, edge_attr_32 = _rec_inputs()

    def _L0_gnn_setup():
        import jax, jax.numpy as jnp
        import numpy as np
        N_NODES = 50000
        N_EDGES = 12500
        D_NODE = 64
        D_EDGE = 32
        D_HID = 128

        def _mlp(x, W1, b1, W2, b2):
            return jax.nn.relu(x @ W1 + b1) @ W2 + b2
        key = jax.random.key(seed)
        ks = jax.random.split(key, 12)
        inp = {'nodes': jax.random.normal(ks[0], (N_NODES, D_NODE), dtype=jnp.float32), 'row': jax.random.randint(ks[1], (N_EDGES,), 0, N_NODES, dtype=jnp.int32), 'col': jax.random.randint(ks[2], (N_EDGES,), 0, N_NODES, dtype=jnp.int32), 'edge_features': jax.random.normal(ks[3], (N_EDGES, D_EDGE), dtype=jnp.float32)}
        d_in_msg = 2 * D_NODE + D_EDGE
        inp['mW1'] = jax.random.normal(ks[4], (d_in_msg, D_HID), dtype=jnp.float32) / np.sqrt(d_in_msg)
        inp['mb1'] = jnp.zeros((D_HID,), dtype=jnp.float32)
        inp['mW2'] = jax.random.normal(ks[5], (D_HID, D_NODE), dtype=jnp.float32) / np.sqrt(D_HID)
        inp['mb2'] = jnp.zeros((D_NODE,), dtype=jnp.float32)
        d_in_upd = 2 * D_NODE
        inp['uW1'] = jax.random.normal(ks[6], (d_in_upd, D_HID), dtype=jnp.float32) / np.sqrt(d_in_upd)
        inp['ub1'] = jnp.zeros((D_HID,), dtype=jnp.float32)
        inp['uW2'] = jax.random.normal(ks[7], (D_HID, D_NODE), dtype=jnp.float32) / np.sqrt(D_HID)
        inp['ub2'] = jnp.zeros((D_NODE,), dtype=jnp.float32)
        return inp
    _L0_gnn_all = _L0_gnn_setup()
    _L0_gnn_in = {k: v for k, v in _L0_gnn_all.items() if k in ('mW1', 'mb1', 'mW2', 'mb2', 'uW1', 'ub1', 'uW2', 'ub2')}
    del _L0_gnn_all

    def _L1_gnn_setup():
        import jax, jax.numpy as jnp
        import numpy as np
        N_NODES = 100000
        N_EDGES = 15625
        IN_DIM = 64
        OUT_DIM = 64
        key = jax.random.key(seed)
        k1, k2, k3, k4, k5 = jax.random.split(key, 5)
        feat = jax.random.normal(k1, (N_NODES, IN_DIM), dtype=jnp.float32)
        src = jax.random.randint(k2, (N_EDGES,), 0, N_NODES, dtype=jnp.int32)
        dst = jax.random.randint(k3, (N_EDGES,), 0, N_NODES, dtype=jnp.int32)
        W = 0.1 * jax.random.normal(k4, (OUT_DIM, IN_DIM), dtype=jnp.float32)
        b = jax.random.normal(k5, (OUT_DIM,), dtype=jnp.float32) * (1.0 / np.sqrt(IN_DIM))
        return {'feat': feat, 'src': src, 'dst': dst, 'W': W, 'b': b}
    _L1_gnn_all = _L1_gnn_setup()
    _L1_gnn_in = {k: v for k, v in _L1_gnn_all.items() if k in ('W', 'b')}
    del _L1_gnn_all

    def _L2_gnn_setup():
        import jax, jax.numpy as jnp
        import numpy as np
        N, E, F = (100000, 25000, 64)
        EPS = 1e-05
        key = jax.random.key(seed)
        k1, k2, k3 = jax.random.split(key, 3)
        h = jax.random.normal(k1, (N, F), dtype=jnp.float32)
        src = jax.random.randint(k2, (E,), 0, N, dtype=jnp.int64)
        dst = jax.random.randint(k3, (E,), 0, N, dtype=jnp.int64)
        gamma = jnp.ones((F,), dtype=jnp.float32)
        beta = jnp.zeros((F,), dtype=jnp.float32)
        return {'h': h, 'src': src, 'dst': dst, 'gamma': gamma, 'beta': beta}
    _L2_gnn_all = _L2_gnn_setup()
    _L2_gnn_in = {k: v for k, v in _L2_gnn_all.items() if k in ('gamma', 'beta')}
    del _L2_gnn_all

    def _L3_gnn_setup():
        import jax, jax.numpy as jnp
        import numpy as np
        N_NODES = 50000
        N_EDGES = 12500
        D_IN = 64
        D_OUT = 64
        key = jax.random.key(seed)
        k1, k2, k3, k4 = jax.random.split(key, 4)
        x = jax.random.normal(k1, (N_NODES, D_IN), dtype=jnp.float32)
        edge_index = jax.random.randint(k2, (2, N_EDGES), 0, N_NODES, dtype=jnp.int64)
        W_edge = jax.random.normal(k3, (2 * D_IN, D_OUT), dtype=jnp.float32) * (1.0 / np.sqrt(2 * D_IN))
        b_edge = jnp.zeros((D_OUT,), dtype=jnp.float32)
        W_res = jax.random.normal(k4, (D_IN, D_OUT), dtype=jnp.float32) * (1.0 / np.sqrt(D_IN))
        b_res = jnp.zeros((D_OUT,), dtype=jnp.float32)
        return {'x': x, 'edge_index': edge_index, 'W_edge': W_edge, 'b_edge': b_edge, 'W_res': W_res, 'b_res': b_res}
    _L3_gnn_all = _L3_gnn_setup()
    _L3_gnn_in = {k: v for k, v in _L3_gnn_all.items() if k in ('W_edge', 'b_edge', 'W_res', 'b_res')}
    del _L3_gnn_all
    return {'x': x, 'src': src, 'dst': dst, 'edge_attr_32': edge_attr_32, 'L0_gnn_mW1': _L0_gnn_in['mW1'], 'L0_gnn_mb1': _L0_gnn_in['mb1'], 'L0_gnn_mW2': _L0_gnn_in['mW2'], 'L0_gnn_mb2': _L0_gnn_in['mb2'], 'L0_gnn_uW1': _L0_gnn_in['uW1'], 'L0_gnn_ub1': _L0_gnn_in['ub1'], 'L0_gnn_uW2': _L0_gnn_in['uW2'], 'L0_gnn_ub2': _L0_gnn_in['ub2'], 'L1_gnn_W': _L1_gnn_in['W'], 'L1_gnn_b': _L1_gnn_in['b'], 'L2_gnn_gamma': _L2_gnn_in['gamma'], 'L2_gnn_beta': _L2_gnn_in['beta'], 'L3_gnn_W_edge': _L3_gnn_in['W_edge'], 'L3_gnn_b_edge': _L3_gnn_in['b_edge'], 'L3_gnn_W_res': _L3_gnn_in['W_res'], 'L3_gnn_b_res': _L3_gnn_in['b_res']}

def reference(x, src, dst, edge_attr_32, L0_gnn_mW1, L0_gnn_mb1, L0_gnn_mW2, L0_gnn_mb2, L0_gnn_uW1, L0_gnn_ub1, L0_gnn_uW2, L0_gnn_ub2, L1_gnn_W, L1_gnn_b, L2_gnn_gamma, L2_gnn_beta, L3_gnn_W_edge, L3_gnn_b_edge, L3_gnn_W_res, L3_gnn_b_res):
    import jax
    import jax.numpy as jnp

    def _L0_gnn_ref(nodes, row, col, edge_features, mW1, mb1, mW2, mb2, uW1, ub1, uW2, ub2):
        import jax, jax.numpy as jnp
        import numpy as np
        N_NODES = 50000
        N_EDGES = 12500
        D_NODE = 64
        D_EDGE = 32
        D_HID = 128

        def _mlp(x, W1, b1, W2, b2):
            return jax.nn.relu(x @ W1 + b1) @ W2 + b2
        msg_in = jnp.concatenate([nodes[row], nodes[col], edge_features], axis=-1)
        messages = _mlp(msg_in, mW1, mb1, mW2, mb2)
        aggregated = jax.ops.segment_sum(messages, col, num_segments=nodes.shape[0])
        upd_in = jnp.concatenate([nodes, aggregated], axis=-1)
        return _mlp(upd_in, uW1, ub1, uW2, ub2)

    def _L1_gnn_ref(feat, src, dst, W, b):
        import jax, jax.numpy as jnp
        import numpy as np
        N_NODES = 100000
        N_EDGES = 15625
        IN_DIM = 64
        OUT_DIM = 64
        msgs = feat[src]
        agg = jax.ops.segment_sum(msgs, dst, num_segments=feat.shape[0])
        return jnp.einsum('nd,od->no', agg, W) + b

    def _L2_gnn_ref(h, src, dst, gamma, beta):
        import jax, jax.numpy as jnp
        import numpy as np
        N, E, F = (100000, 25000, 64)
        EPS = 1e-05
        n_nodes, n_feat = h.shape
        one = jnp.ones_like(src, dtype=h.dtype)
        deg = jax.ops.segment_sum(one, dst, num_segments=n_nodes)
        src_h = h[src]
        s1 = h.sum(-1) + jax.ops.segment_sum(src_h.sum(-1), dst, num_segments=n_nodes)
        s2 = (h * h).sum(-1) + jax.ops.segment_sum((src_h * src_h).sum(-1), dst, num_segments=n_nodes)
        n_elem = (deg + 1.0) * n_feat
        mean = s1 / n_elem
        var = (s2 - n_elem * mean * mean) / (n_elem - 1.0)
        std = jnp.sqrt(jnp.clip(var, 0.0))
        has_msg = deg > 0
        mean = jnp.where(has_msg, mean, 0.0)
        std = jnp.where(has_msg, std, 0.0)
        norm_h = (h - mean[:, None]) / (std[:, None] + EPS)
        return gamma * norm_h + beta

    def _L3_gnn_ref(x, edge_index, W_edge, b_edge, W_res, b_res):
        import jax, jax.numpy as jnp
        import numpy as np
        N_NODES = 50000
        N_EDGES = 12500
        D_IN = 64
        D_OUT = 64
        src, dst = (edge_index[0], edge_index[1])
        x_i = x[dst]
        x_j = x[src]
        msg_in = jnp.concatenate([x_i, x_j - x_i], axis=-1)
        msg = jax.nn.relu(msg_in @ W_edge + b_edge)
        agg = jax.ops.segment_max(msg, dst, num_segments=x.shape[0])
        agg = jnp.where(jnp.isfinite(agg), agg, 0.0)
        return agg + x @ W_res + b_res
    edge_index = jnp.stack([src, dst])
    x = _layernorm(x + _L0_gnn_ref(x, src, dst, edge_attr_32, L0_gnn_mW1, L0_gnn_mb1, L0_gnn_mW2, L0_gnn_mb2, L0_gnn_uW1, L0_gnn_ub1, L0_gnn_uW2, L0_gnn_ub2), axis=-1)
    x = _layernorm(x + _L1_gnn_ref(x, src, dst, L1_gnn_W, L1_gnn_b), axis=-1)
    x = _layernorm(x + _L2_gnn_ref(x, src, dst, L2_gnn_gamma, L2_gnn_beta), axis=-1)
    x = _layernorm(x + _L3_gnn_ref(x, edge_index, L3_gnn_W_edge, L3_gnn_b_edge, L3_gnn_W_res, L3_gnn_b_res), axis=-1)
    return x

_drawn_inputs = setup_inputs


def setup_inputs(seed=0):
    import zlib

    import numpy as np

    out = dict(_drawn_inputs(seed))
    spreads = {'L0_gnn_mb1': (0.0, 0.749),
     'L0_gnn_mb2': (0.0, 0.482),
     'L0_gnn_ub1': (0.0, 0.1),
     'L0_gnn_ub2': (0.0, 0.1),
     'L2_gnn_gamma': (1.0, 0.2),
     'L2_gnn_beta': (0.0, 0.351),
     'L3_gnn_b_edge': (0.0, 0.474),
     'L3_gnn_b_res': (0.0, 0.1)}
    factors = {}
    for name, (base, spread) in spreads.items():
        noise = np.random.default_rng([zlib.crc32(name.encode()), seed]).standard_normal(out[name].shape)
        drawn = base * np.exp(spread * noise) if base else spread * noise
        out[name] = jnp.asarray(drawn.astype(out[name].dtype))
    for name, factor in factors.items():
        out[name] = (out[name] * factor).astype(out[name].dtype)
    return out
```

```python
def build_gnn(nc, x, src, dst, edge_attr, mW1, mb1, mW2, mb2, uW1, ub1, uW2, ub2,
              W1, b1, gamma, beta, W_edge, b_edge, W_res, b_res, out):
    import concourse.bass as bass
    from concourse import mybir
    from contextlib import ExitStack

    f32 = mybir.dt.float32
    i32 = mybir.dt.int32
    ALU = mybir.AluOpType
    ACT = mybir.ActivationFunctionType
    AX = mybir.AxisListType

    N, D = x.shape
    E, DE = edge_attr.shape
    HID = mW1.shape[1]
    P = 125
    D2 = 2 * D
    CT = 4
    CE = CT * P
    NT = E // P
    STEPS = E // (2 * CE)
    R = 8
    BLOCKS = N // (P * R)
    HALF = NT // 2
    PA = 112
    EPS = 1e-5
    STD_EPS_INV = 1.0 / EPS
    FAR = 1048576.0
    N_LOADS = 23
    STAT_STEPS = 17
    LOW = -3.0e38
    assert BLOCKS == 4 * STEPS and NT == 2 * HALF and D2 == 128 and HID == 128

    tables = [nc.dram_tensor(f"edge_rows_{l}", (E, D2), f32, kind="Internal").ap() for l in range(3)]
    slot_table = nc.dram_tensor("slot_table", (N, 1), f32, kind="Internal").ap()
    same_row = nc.dram_tensor("same_row", (1, E), f32, kind="Internal").ap()
    forget_row = nc.dram_tensor("forget_row", (1, E), f32, kind="Internal").ap()
    gather_view = [t.rearrange("e (k d) -> (e k) d", k=2) for t in tables]

    ctx = ExitStack()
    with ctx:
        def sb(name, shape, dt=f32):
            return ctx.enter_context(nc.sbuf_tensor(name, shape, dt))

        def sem(name):
            return ctx.enter_context(nc.semaphore(name))

        ident = sb("ident", [128, 128])
        ones_row = sb("ones_row", [1, CE])
        ones2 = sb("ones2", [128, 2])
        center2 = sb("center2", [128, 128])
        w_upd_top = sb("w_upd_top", [128, 128])
        w_upd_bot = sb("w_upd_bot", [128, 128])
        w_upd_agg = sb("w_upd_agg", [128, 128])
        w_out_a = sb("w_out_a", [128, 128])
        w_out_b = sb("w_out_b", [128, 128])
        w_msg_x = sb("w_msg_x", [128, 128])
        w_msg_e = sb("w_msg_e", [128, 128])
        w_msg_2 = sb("w_msg_2", [128, D])
        w_l1 = sb("w_l1", [128, 128])
        w_gamma = sb("w_gamma", [128, 128])
        w_l2_dense = sb("w_l2_dense", [128, 128])
        w_l3 = sb("w_l3", [128, 128])
        w_xi = sb("w_xi", [128, D])
        w_xj = sb("w_xj", [128, D])
        w_raw = sb("w_raw", [128, 4, D])
        row_mean = sb("row_mean", [128, 8])
        bias = [sb(f"bias_{l}", [128, 8, D]) for l in range(4)]
        bias_raw = sb("bias_raw", [128, 4, D])
        col_mb1 = sb("col_mb1", [128, 1])
        col_ub1 = sb("col_ub1", [128, 1])
        col_mb2 = sb("col_mb2", [D, 1])
        col_be = sb("col_be", [D, 1])
        col_gamma = sb("col_gamma", [128, 1])
        col_eps = sb("col_eps", [128, 1])
        col_zero = sb("col_zero", [128, 1])
        minus_one = sb("minus_one", [P, N // P])

        dst_i = sb("dst_i", [HALF, 2, P], i32)
        src_i = sb("src_i", [HALF, 2, P], i32)
        prev_i = sb("prev_i", [HALF, 2, P], i32)
        next_i = sb("next_i", [HALF, 2, P], i32)
        dst_f = sb("dst_f", [HALF, 2, P])
        src_f = sb("src_f", [HALF, 2, P])
        near_f = sb("near_f", [HALF, 2, P])
        last_f = sb("last_f", [HALF, 2, P])
        same_f = sb("same_f", [HALF, 2, P])
        forget_f = sb("forget_f", [HALF, 2, P])
        dst_col = sb("dst_col", [P, NT], i32)
        src_col = sb("src_col", [P, NT], i32)
        last_col = sb("last_col", [P, NT], i32)
        source_row = sb("source_row", [P, NT], i32)
        edge2_i = sb("edge2_i", [P, NT], i32)
        edge2 = sb("edge2", [P, NT])

        d_rows = sb("d_rows", [P, R * D])
        d_rowsT = sb("d_rowsT", [128, CE])
        d_hid = [sb(f"d_hid{h}", [128, CE]) for h in range(2)]
        d_u = sb("d_u", [P, R, D])
        d_sq = sb("d_sq", [P, R, D])
        d_x = sb("d_x", [P, R, D])
        d_out = sb("d_out", [P, R, D])
        d_var = sb("d_var", [P, R])
        d_std = sb("d_std", [P, R])
        d_inv = sb("d_inv", [P, R])

        def two(name, shape, dt=f32):
            return [sb(f"{name}{c}", shape, dt) for c in range(2)]

        e_idx = two("e_idx", [P, 3 * CT], i32)
        e_val = two("e_val", [P, CT])
        e_slot = two("e_slot", [P, CT])
        e_fix = two("e_fix", [P, CT])
        e_rows = two("e_rows", [P, CT, D2])
        e_src = two("e_src", [P, CT, D2])
        e_attr = two("e_attr", [P, CT, DE])
        e_mask = two("e_mask", [128, CE])
        e_rowsT = two("e_rowsT", [128, CE])
        e_srcT = two("e_srcT", [128, CE])
        e_hid = two("e_hid", [128, CE])
        e_hidS = two("e_hidS", [128, CE])
        e_msg = two("e_msg", [D, CE])
        e_agg = two("e_agg", [128, CE])
        e_deg = two("e_deg", [1, CE])
        e_u = two("e_u", [P, 2 * CT, D])
        e_sq = two("e_sq", [P, 2 * CT, D])
        e_new = two("e_new", [P, 2 * CT, D])
        e_var = two("e_var", [P, 2 * CT])
        e_std = two("e_std", [P, 2 * CT])
        e_inv = two("e_inv", [P, 2 * CT])
        e_small = two("e_small", [P, 12, CT])
        e_mean2 = two("e_mean2", [P, CT, 2])
        e_rstd2 = two("e_rstd2", [P, CT, 2])

        bank = [ctx.enter_context(nc.psum_tensor(f"bank{i}", [128, 512], f32)) for i in range(8)]
        d_bank = bank[0:3]
        e_bank = [bank[3:5], bank[5:7]]
        s_bank = bank[7]

        k_zero = sem("k_zero")
        k_ident = sem("k_ident")
        ld_w = sem("ld_w")
        ld_i = sem("ld_i")
        k_dve = sem("k_dve")
        k_flags = sem("k_flags")
        k_tr = sem("k_tr")
        k_idx = sem("k_idx")
        k_ready = sem("k_ready")
        flags_out = sem("flags_out")
        slots_clear = sem("slots_clear")
        out_done = sem("out_done")

        def pair(name):
            return [sem(f"{name}_{c}") for c in range(2)]

        slots_set = pair("slots_set")
        slot_idx = pair("slot_idx")
        slot_got = pair("slot_got")
        slot_fix = pair("slot_fix")
        src_known = pair("src_known")

        d_load, d_tr, d_ev, d_hm, d_r0, d_r1, d_mm, d_us, d_sqs, d_vs, d_sd, d_iv, d_xs, d_store = [
            sem(f"dense_{n}") for n in ("loaded", "transposed", "evacuated", "hidden", "relu0", "relu1", "product",
                                        "biased", "squared", "summed", "std", "inverse", "normed", "stored")]

        class Layer:
            pass

        L = [Layer() for _ in range(4)]
        rowsT = pair("rowsT")
        prod = pair("prod")
        biased = pair("biased")
        sq = pair("sq")
        summed = pair("summed")
        std = pair("std")
        inv = pair("inv")
        new = pair("new")
        for l, y in enumerate(L):
            y.n0 = l * STEPS
            y.idx = pair(f"idx{l}")
            y.got = pair(f"got{l}")
            y.flag = pair(f"flag{l}")
            y.tr = pair(f"tr{l}")
            y.scan = pair(f"scan{l}")
            y.stored = pair(f"stored{l}")
            if l == 0:
                y.attr = pair("attr0")
            else:
                y.rows = pair(f"rows{l}")
        attr_T = pair("attr_T")
        msg_hid = pair("msg_hid"); msg_relu = pair("msg_relu")
        msg_out = pair("msg_out"); msg_sb = pair("msg_sb")
        upd_hid = pair("upd_hid"); upd_reluD = pair("upd_reluD"); upd_reluS = pair("upd_reluS")
        src_sq = pair("src_sq"); own_sq = pair("own_sq")
        sums = pair("sums"); stat = pair("stat"); raw_std = pair("raw_std"); var_ok = pair("var_ok")
        scaled = pair("scaled"); scaled_tr = pair("scaled_tr"); scaled_T = pair("scaled_T")
        srcT3 = pair("srcT3"); vz = pair("vz"); z_in = pair("z_in"); z_relu = pair("z_relu")

        block = ctx.enter_context(nc.Block())

        def in_turn(*chains):
            live = list(chains)
            while live:
                for chain in list(live):
                    if next(chain, "end") == "end":
                        live.remove(chain)

        base = {0: 0, "slots": STEPS, 1: 2 * STEPS, 2: 3 * STEPS}

        def phases(eng, dense, layers, slots):
            def step0(t):
                in_turn(layers[0](t, 0), layers[0](t, 1), dense(base[0] + t))

            def step_slots(t):
                if slots is not None:
                    slots(t)
                in_turn(dense(base["slots"] + t))

            def step1(t):
                in_turn(layers[1](t, 0), layers[1](t, 1), dense(base[1] + t))

            def step2(t):
                in_turn(layers[2](t, 0), layers[2](t, 1), dense(base[2] + t))

            def step3(t):
                in_turn(layers[3](t, 0), layers[3](t, 1))

            for step in (step0, step_slots, step1, step2, step3):
                step(0)
                with eng.Fori(1, STEPS) as t:
                    step(t)

        def again(eng, s, per, t):
            if not isinstance(t, int) or t > 0:
                eng.wait_ge(s, per * t)

        def stepper(eng, s, per, t):
            done = [0]

            def step(ins):
                done[0] += 1
                ins.then_inc(s, 1)
                eng.wait_ge(s, per * t + done[0])
            return step

        def rows_dma(eng, o, i, s):
            eng.dma_start(o[0:PA], i[0:PA]).then_inc(s, 16)
            eng.dma_start(o[PA:P], i[PA:P]).then_inc(s, 16)

        def dense_rows(a, n):
            return a[bass.ds(n * (P * R), P * R), :].rearrange("(p r) d -> p r d", r=R)

        def edge_cols(a, t, c):
            return a[0:1, bass.ds(t * (2 * CE) + c * CE, CE)]

        def edge_rows(a, t, c):
            return a[bass.ds(t * (2 * CE) + c * CE, CE), :].rearrange("(j p) d -> p j d", p=P)

        def tile_cols(a, t, c):
            return a[:, bass.ds(t * (2 * CT) + c * CT, CT)]

        @block.sync
        def _(sp):
            def halves(a, lo):
                return a[lo:lo + 2 * HALF * P].rearrange("(g t p) -> t g p", g=2, p=P)

            sp.wait_ge(k_zero, 1)
            sp.dma_start(dst_i[:, :, :], halves(dst, 0)).then_inc(ld_i, 16)
            sp.dma_start(src_i[:, :, :], halves(src, 0)).then_inc(ld_i, 16)
            one = dst[0:P - 1].rearrange("(a p) -> a p", a=1)
            sp.dma_start(prev_i[0:1, 0, 1:P], one).then_inc(ld_i, 16)
            sp.dma_start(prev_i[1:HALF, 0, :], dst[P - 1:HALF * P - 1].rearrange("(t p) -> t p", p=P)).then_inc(ld_i, 16)
            sp.dma_start(prev_i[:, 1, :], dst[HALF * P - 1:E - 1].rearrange("(t p) -> t p", p=P)).then_inc(ld_i, 16)
            sp.dma_start(next_i[:, 0, :], dst[1:HALF * P + 1].rearrange("(t p) -> t p", p=P)).then_inc(ld_i, 16)
            sp.dma_start(next_i[0:HALF - 1, 1, :], dst[HALF * P + 1:E - P + 1].rearrange("(t p) -> t p", p=P)).then_inc(ld_i, 16)
            one = dst[E - P + 1:E].rearrange("(a p) -> a p", a=1)
            sp.dma_start(next_i[HALF - 1:HALF, 1, 0:P - 1], one).then_inc(ld_i, 16)
            sp.dma_start(slot_table.rearrange("(p k) o -> p (k o)", p=P), minus_one[:, :]).then_inc(slots_clear, 16)
            col = lambda a: a.rearrange("(p o) -> p o", o=1)
            for o, i in (
                (w_upd_top[0:D, :], uW1[0:D, :]), (w_upd_bot[D:D2, :], uW1[0:D, :]),
                (w_upd_agg[0:D, :], uW1[D:D2, :]),
                (w_msg_x[0:D, :], mW1[D:D2, :]), (w_msg_x[D:D2, :], mW1[0:D, :]),
                (w_msg_e[0:DE, :], mW1[D2:D2 + DE, :]), (w_msg_2[:, :], mW2),
                (w_raw[:, 0, :], uW2), (w_raw[0:D, 1, :], W1),
                (w_raw[0:D, 2, :], W_res), (w_raw[D:D2, 2, :], W_res),
                (w_xi[0:D, :], W_edge[0:D, :]), (w_xj[0:D, :], W_edge[D:D2, :]),
                (col_mb1[:, :], col(mb1)), (col_ub1[:, :], col(ub1)), (col_mb2[:, :], col(mb2)),
                (col_be[:, :], col(b_edge)), (col_gamma[0:D, :], col(gamma)), (col_gamma[D:D2, :], col(gamma)),
                (bias_raw[:, 0, :], ub2.partition_broadcast(128)), (bias_raw[:, 1, :], b1.partition_broadcast(128)),
                (bias_raw[:, 2, :], beta.partition_broadcast(128)), (bias_raw[:, 3, :], b_res.partition_broadcast(128)),
            ):
                sp.dma_start(o, i).then_inc(ld_w, 16)
            sp.wait_ge(k_flags, 1)
            sp.dma_start(halves(same_row[0, :], 0), same_f[:, :, :]).then_inc(flags_out, 16)
            sp.dma_start(halves(forget_row[0, :], 0), forget_f[:, :, :]).then_inc(flags_out, 16)
            sp.wait_ge(flags_out, 32)

            def load_dense(n):
                again(sp, d_tr, 3, n)
                rows_dma(sp, d_rows[:, :].rearrange("p (r d) -> p r d", r=R), dense_rows(x, n), d_load)

            def store_dense(n):
                sp.wait_ge(d_xs, 4 * n + 4)
                rows_dma(sp, dense_rows(out, n), d_out, d_store)

            def load(l, t, c):
                y = L[l]
                again(sp, y.scan[c], 1, t)
                flag = forget_row if l == 3 else same_row
                sp.dma_start(e_mask[c][:, :], edge_cols(flag, t, c)[0, :].partition_broadcast(128)).then_inc(y.flag[c], 16)
                again(sp, y.tr[c], 1, t)
                if l == 0:
                    rows_dma(sp, e_attr[c], edge_rows(edge_attr, t, c), y.attr[c])
                else:
                    if l == 2:
                        again(sp, scaled[c], 1, t)
                    rows_dma(sp, e_rows[c], edge_rows(tables[l - 1], t, c), y.rows[c])

            def store(l, t, c):
                y = L[l]
                sp.wait_ge(new[c], y.n0 + t + 1)
                rows = e_new[c][:, :, :].rearrange("p (j k) d -> p j (k d)", k=2)
                rows_dma(sp, edge_rows(tables[l], t, c), rows, y.stored[c])

            for l in range(4):
                def loads(t, l=l):
                    for c in range(2):
                        load(l, t, c)
                    if l < 3:
                        load_dense(base[l] + t)

                def stores(t, l=l):
                    if l < 3:
                        for c in range(2):
                            store(l, t, c)
                        store_dense(base[l] + t)

                if l > 0:
                    for c in range(2):
                        sp.wait_ge(L[l - 1].stored[c], 32 * STEPS)
                loads(0)
                with sp.Fori(1, STEPS) as t:
                    loads(t)
                    stores(t - 1)
                stores(STEPS - 1)
                if l == 0:
                    load_dense(STEPS)
                    with sp.Fori(1, STEPS) as t:
                        load_dense(STEPS + t)
                        store_dense(STEPS + t - 1)
                    store_dense(2 * STEPS - 1)
            sp.wait_ge(d_store, 32 * BLOCKS)
            for c in range(2):
                sp.wait_ge(slots_set[c], 16 * CT * STEPS)
                sp.wait_ge(L[3].stored[c], 16 * CT * STEPS)
            sp.wait_ge(slots_clear, 16)

        @block.gpsimd
        def _(pool):
            pool.memset(prev_i[:, :, :], -1)
            pool.memset(next_i[:, :, :], -1)
            pool.memset(minus_one[:, :], -1.0)
            pool.memset(ones_row[:, :], 1.0)
            pool.memset(ones2[:, :], 0.0)
            pool.memset(col_eps[:, :], EPS)
            for w in (w_upd_top, w_upd_bot, w_upd_agg, w_out_a, w_out_b, w_msg_e, w_l1, w_l2_dense, w_l3,
                      w_gamma, center2, w_xi, w_xj):
                pool.memset(w[:, :], 0.0)
            for c in range(2):
                pool.memset(e_agg[c][:, :], 0.0)
                pool.memset(e_srcT[c][:, :], 0.0)
                pool.memset(e_hid[c][:, :], 0.0)
                pool.memset(e_deg[c][:, :], 0.0)
                pool.memset(e_mean2[c][:, :, :], 0.0)
                pool.memset(e_rstd2[c][:, :, :], STD_EPS_INV)
            pool.memset(ident[:, :], 0.0).then_inc(k_zero, 1)
            pool.iota(edge2_i[:, :], pattern=[[2 * P, NT]], base=0, channel_multiplier=2).then_inc(k_ident, 1)
            pool.wait_ge(k_zero, 1)
            pool.affine_select(out=ident[:, :], in_=ident[:, :], compare_op=ALU.not_equal, fill=1.0, base=0,
                               pattern=[[-1, 128]], channel_multiplier=1).then_inc(k_ident, 1)
            pool.wait_ge(k_idx, 1)

            def copy_idx(c, t, s, parts):
                for k, table in enumerate(parts):
                    last = pool.tensor_copy(e_idx[c][:, k * CT:(k + 1) * CT], tile_cols(table, t, c))
                last.then_inc(s, 1)
                pool.wait_ge(s, t + 1)
                pool.nop(nofuse=True)

            def gather(o, table, c, k, s):
                pool.indirect_dma_start(out=o, out_offset=None, in_=table, in_offset=bass.IndirectOffsetOnAxis(
                    ap=e_idx[c][:, k:k + 1], axis=0)).then_inc(s, 16)

            def scatter(table, i, c, k, s):
                pool.indirect_dma_start(out=table, out_offset=bass.IndirectOffsetOnAxis(
                    ap=e_idx[c][:, k:k + 1], axis=0), in_=i, in_offset=None,
                    bounds_check=N - 1, oob_is_err=False).then_inc(s, 16)

            def layer0(t):
                for c in range(2):
                    again(pool, L[0].tr[c], 1, t)
                    again(pool, slots_set[c], 16 * CT, t)
                    pool.tensor_copy(e_val[c][:, :], tile_cols(edge2, t, c))
                    copy_idx(c, t, L[0].idx[c], (dst_col, src_col, last_col))
                    for j in range(CT):
                        gather(e_rows[c][:, j, 0:D], x, c, j, L[0].got[c])
                        gather(e_rows[c][:, j, D:D2], x, c, CT + j, L[0].got[c])
                    for j in range(CT):
                        scatter(slot_table, e_val[c][:, j:j + 1], c, 2 * CT + j, slots_set[c])

            def slots(t):
                for c in range(2):
                    again(pool, src_known[c], 1, t)
                    copy_idx(c, t, slot_idx[c], (src_col,))
                    for j in range(CT):
                        gather(e_slot[c][:, j:j + 1], slot_table, c, j, slot_got[c])

            def sources(l, t):
                for c in range(2):
                    again(pool, L[l].tr[c], 1, t)
                    copy_idx(c, t, L[l].idx[c], (source_row, last_col))
                    for j in range(CT):
                        gather(e_src[c][:, j, 0:D], gather_view[l - 1], c, j, L[l].got[c])

            def results(t):
                for c in range(2):
                    pool.wait_ge(new[c], L[3].n0 + t + 1)
                    pool.nop(nofuse=True)
                    for j in range(CT):
                        scatter(out, e_new[c][:, j, :], c, CT + j, L[3].stored[c])

            pool.wait_ge(slots_clear, 16)
            layer0(0)
            with pool.Fori(1, STEPS) as t:
                layer0(t)
            for c in range(2):
                pool.wait_ge(slots_set[c], 16 * CT * STEPS)
            slots(0)
            with pool.Fori(1, STEPS) as t:
                slots(t)
            for c in range(2):
                pool.wait_ge(src_known[c], STEPS)
            for l in (1, 2):
                for c in range(2):
                    pool.wait_ge(L[l - 1].stored[c], 32 * STEPS)
                sources(l, 0)
                with pool.Fori(1, STEPS) as t:
                    sources(l, t)
            for c in range(2):
                pool.wait_ge(L[2].stored[c], 32 * STEPS)
            pool.wait_ge(d_store, 32 * BLOCKS)
            sources(3, 0)
            results(0)
            with pool.Fori(1, STEPS) as t:
                for c in range(2):
                    pool.wait_ge(L[3].stored[c], 16 * CT * t)
                sources(3, t)
                results(t)

        @block.tensor
        def _(pe):
            pe.wait_ge(k_flags, 1)
            for k, a in enumerate((dst_f, src_f, last_f)):
                for g in range(2):
                    pe.transpose(bank[k][0:P, g * HALF:(g + 1) * HALF], a[:, g, :], ident[0:HALF, 0:HALF])
            pe.wait_ge(ld_w, 16 * N_LOADS)
            pe.transpose(bank[3][0:D, 0:D], w_raw[0:D, 1, :], ident[0:D, 0:D]).then_inc(k_tr, 1)
            pe.wait_ge(k_ready, 1)

            def pair_transposes(o, rows, s):
                for q in range(CT):
                    last = pe.transpose(o[:, q * P:(q + 1) * P], rows(q), ident[0:P, 0:P])
                if s is not None:
                    last.then_inc(s, 1)
                return last

            def products(o, width, terms, s):
                for q in range(CT):
                    for k, (a, w) in enumerate(terms):
                        last = pe.matmul(o[0:P, q * width:(q + 1) * width], a[:, q * P:(q + 1) * P], w,
                                         start=k == 0, stop=k == len(terms) - 1)
                last.then_inc(s, 1)

            def dense(n):
                b = d_bank
                pe.wait_ge(d_load, 32 * n + 32)
                again(pe, d_us, 4, n)
                pair_transposes(b[0], lambda q: d_rows[:, q * D2:(q + 1) * D2], d_tr)
                yield
                pe.wait_ge(d_ev, 3 * n + 1)
                pe.matmul(b[1][:, 0:CE], w_upd_top[:, :], d_rowsT[:, :], start=True, stop=True)
                pe.matmul(b[2][:, 0:CE], w_upd_bot[:, :], d_rowsT[:, :], start=True, stop=True).then_inc(d_hm, 1)
                yield
                pe.wait_ge(d_r0, n + 1)
                pe.wait_ge(d_r1, n + 1)
                products(b[0], D2, ((d_hid[0], w_out_a[:, :]), (d_hid[1], w_out_b[:, :]), (d_rowsT, center2[:, :])), d_mm)
                yield
                yield
                yield
                pe.wait_ge(d_xs, 4 * n + 2)
                pair_transposes(b[1], lambda q: d_x[:, 2 * q:2 * q + 2, :].rearrange("p r d -> p (r d)"), d_tr)
                yield
                pe.wait_ge(d_ev, 3 * n + 2)
                products(b[0], D2, ((d_rowsT, w_l2_dense[:, :]),), d_mm)
                yield
                yield
                pe.wait_ge(d_xs, 4 * n + 3)
                pair_transposes(b[1], lambda q: d_x[:, 2 * q:2 * q + 2, :].rearrange("p r d -> p (r d)"), d_tr)
                yield
                pe.wait_ge(d_ev, 3 * n + 3)
                products(b[0], D2, ((d_rowsT, w_l3[:, :]),), d_mm)

            def layer0(t, c):
                y, (b0, b1) = L[0], e_bank[c]
                pe.wait_ge(y.got[c], 32 * CT * t + 32 * CT)
                again(pe, biased[c], 1, y.n0 + t)
                pair_transposes(b0, lambda q: e_rows[c][:, q, :], None)
                pe.wait_ge(y.attr[c], 32 * t + 32)
                for q in range(CT):
                    last = pe.transpose(b1[0:DE, q * P:(q + 1) * P], e_attr[c][:, q, :], ident[0:P, 0:P])
                last.then_inc(y.tr[c], 1)
                yield
                pe.wait_ge(rowsT[c], y.n0 + t + 1)
                pe.wait_ge(attr_T[c], t + 1)
                pe.matmul(b0[:, 0:CE], w_msg_x[:, :], e_rowsT[c][:, :], start=True, stop=False)
                pe.matmul(b0[:, 0:CE], w_msg_e[:, :], e_srcT[c][:, :], start=False, stop=True).then_inc(msg_hid[c], 1)
                yield
                pe.wait_ge(msg_relu[c], t + 1)
                pe.matmul(b1[0:D, 0:CE], w_msg_2[:, :], e_hid[c][:, :], start=True, stop=True).then_inc(msg_out[c], 1)
                yield
                pe.wait_ge(y.scan[c], t + 1)
                pe.matmul(b0[:, 0:CE], w_upd_top[:, :], e_rowsT[c][:, :], start=True, stop=False)
                pe.matmul(b0[:, 0:CE], w_upd_agg[:, :], e_agg[c][:, :], start=False, stop=True)
                pe.matmul(b1[:, 0:CE], w_upd_bot[:, :], e_rowsT[c][:, :], start=True, stop=True).then_inc(upd_hid[c], 1)
                yield
                pe.wait_ge(upd_reluD[c], t + 1)
                pe.wait_ge(upd_reluS[c], t + 1)
                products(b0, D2, ((e_hid[c], w_out_a[:, :]), (e_hidS[c], w_out_b[:, :]), (e_rowsT[c], center2[:, :])), prod[c])

            def transpose_sources(y, b1, c, t, width):
                pe.wait_ge(y.got[c], 16 * CT * t + 16 * CT)
                pe.nop(nofuse=True)
                for q in range(CT):
                    last = pe.transpose(b1[0:width, q * P:(q + 1) * P], e_src[c][:, q, 0:width], ident[0:P, 0:P])
                last.then_inc(y.tr[c], 1)

            def transpose_rows(y, b0, c, t):
                pe.wait_ge(y.rows[c], 32 * t + 32)
                again(pe, biased[c], 1, y.n0 + t)
                pair_transposes(b0, lambda q: e_rows[c][:, q, :], None)

            def layer1(t, c):
                y, (b0, b1) = L[1], e_bank[c]
                transpose_rows(y, b0, c, t)
                transpose_sources(y, b1, c, t, D)
                yield
                pe.wait_ge(rowsT[c], y.n0 + t + 1)
                pe.wait_ge(y.scan[c], t + 1)
                products(b0, D2, ((e_rowsT[c], center2[:, :]), (e_agg[c], w_l1[:, :])), prod[c])

            def layer2(t, c):
                y, (b0, b1) = L[2], e_bank[c]
                transpose_rows(y, b0, c, t)
                pe.wait_ge(src_sq[c], t + 1)
                transpose_sources(y, b1, c, t, D2)
                yield
                pe.wait_ge(y.scan[c], t + 1)
                for q in range(CT):
                    pe.matmul(b1[0:P, 2 * q:2 * q + 2], e_agg[c][:, q * P:(q + 1) * P], ones2[:, :], start=True, stop=True)
                for q in range(CT):
                    last = pe.matmul(b1[0:P, 2 * CT + q:2 * CT + q + 1], e_deg[c][0:1, q * P:(q + 1) * P],
                                     ones_row[0:1, 0:1], start=True, stop=True)
                last.then_inc(sums[c], 1)
                yield
                yield
                pe.wait_ge(scaled[c], t + 1)
                pair_transposes(b1, lambda q: e_sq[c][:, 2 * q:2 * q + 2, :].rearrange("p r d -> p (r d)"), scaled_tr[c])
                yield
                pe.wait_ge(rowsT[c], y.n0 + t + 1)
                pe.wait_ge(scaled_T[c], t + 1)
                products(b0, D2, ((e_rowsT[c], center2[:, :]), (e_srcT[c], w_gamma[:, :])), prod[c])

            def layer3(t, c):
                y, (b0, b1) = L[3], e_bank[c]
                transpose_rows(y, b0, c, t)
                transpose_sources(y, b1, c, t, D)
                yield
                pe.wait_ge(rowsT[c], y.n0 + t + 1)
                pe.wait_ge(srcT3[c], t + 1)
                pe.matmul(b1[0:D, 0:CE], w_xj[:, :], e_srcT[c][:, :], start=True, stop=True)
                pe.matmul(b0[0:D, 0:CE], w_xi[:, :], e_rowsT[c][:, :], start=True, stop=True).then_inc(vz[c], 1)
                yield
                pe.wait_ge(z_relu[c], t + 1)
                products(b0, D, ((e_rowsT[c], w_l3[:, 0:D]), (e_hid[c], center2[:, 0:D])), prod[c])

            phases(pe, dense, (layer0, layer1, layer2, layer3), None)

        @block.scalar
        def _(act):
            act.wait_ge(k_ready, 1)

            def norm(o_sq, u, var, o_std, biased, squared, summed, stded, k):
                act.wait_ge(biased, k)
                act.activation(o_sq, u, ACT.Square).then_inc(squared, 1)
                yield
                act.wait_ge(summed, k)
                act.activation(o_std, var, ACT.Sqrt, bias=col_eps[0:P, :], scale=1.0 / D).then_inc(stded, 1)

            def dense(n):
                def norm_d(k):
                    return norm(d_sq[:, :, :], d_u[:, :, :], d_var[:, :], d_std[:, :], d_us, d_sqs, d_vs, d_sd, 4 * n + k)

                def evacuate(b, k):
                    act.wait_ge(d_tr, 3 * n + k)
                    act.activation(d_rowsT[:, :], b[:, 0:CE], ACT.Copy).then_inc(d_ev, 1)

                again(act, d_mm, 3, n)
                evacuate(d_bank[0], 1)
                yield
                act.wait_ge(d_hm, n + 1)
                act.activation(d_hid[0][:, :], d_bank[1][:, 0:CE], ACT.Relu, bias=col_ub1[:, :]).then_inc(d_r0, 1)
                yield
                yield from norm_d(1)
                yield from norm_d(2)
                yield
                evacuate(d_bank[1], 2)
                yield
                yield from norm_d(3)
                yield
                evacuate(d_bank[1], 3)
                yield
                yield from norm_d(4)

            def tail(l, t, c, width):
                y = L[l]
                yield from norm(e_sq[c][:, 0:width, :], e_u[c][:, 0:width, :], e_var[c][:, 0:width], e_std[c][:, 0:width],
                                biased[c], sq[c], summed[c], std[c], y.n0 + t + 1)

            def rows_T(l, t, c):
                act.wait_ge(L[l].tr[c], t + 1)
                act.activation(e_rowsT[c][:, :], e_bank[c][0][:, 0:CE], ACT.Copy).then_inc(rowsT[c], 1)

            def layer0(t, c):
                rows_T(0, t, c)
                yield
                act.wait_ge(msg_hid[c], t + 1)
                act.activation(e_hid[c][:, :], e_bank[c][0][:, 0:CE], ACT.Relu, bias=col_mb1[:, :]).then_inc(msg_relu[c], 1)
                yield
                act.wait_ge(msg_out[c], t + 1)
                act.activation(e_msg[c][:, :], e_bank[c][1][0:D, 0:CE], ACT.Identity, bias=col_mb2[:, :]).then_inc(msg_sb[c], 1)
                yield
                act.wait_ge(upd_hid[c], t + 1)
                act.activation(e_hid[c][:, :], e_bank[c][0][:, 0:CE], ACT.Relu, bias=col_ub1[:, :]).then_inc(upd_reluD[c], 1)
                yield
                yield from tail(0, t, c, 2 * CT)

            def layer1(t, c):
                rows_T(1, t, c)
                yield
                yield from tail(1, t, c, 2 * CT)

            def layer2(t, c):
                act.wait_ge(L[2].got[c], 16 * CT * t + 16 * CT)
                act.activation(e_src[c][:, :, D:D2], e_src[c][:, :, 0:D], ACT.Square).then_inc(src_sq[c], 1)
                act.wait_ge(L[2].rows[c], 32 * t + 32)
                act.activation(e_u[c][:, 0:CT, :], e_rows[c][:, :, 0:D], ACT.Square).then_inc(own_sq[c], 1)
                rows_T(2, t, c)
                yield
                act.wait_ge(var_ok[c], t + 1)
                act.activation(e_small[c][:, 10, :], e_small[c][:, 6, :], ACT.Sqrt).then_inc(raw_std[c], 1)
                yield
                yield
                act.wait_ge(scaled_tr[c], t + 1)
                act.activation(e_srcT[c][:, :], e_bank[c][1][:, 0:CE], ACT.Copy).then_inc(scaled_T[c], 1)
                yield
                yield from tail(2, t, c, 2 * CT)

            def layer3(t, c):
                rows_T(3, t, c)
                yield
                act.wait_ge(z_in[c], t + 1)
                act.activation(e_hid[c][0:D, :], e_msg[c][:, :], ACT.Relu, bias=col_be[:, :]).then_inc(z_relu[c], 1)
                yield
                yield from tail(3, t, c, CT)

            phases(act, dense, (layer0, layer1, layer2, layer3), None)

        @block.vector
        def _(dve):
            link = stepper(dve, k_dve, 0, 0)
            dve.wait_ge(k_ident, 2)
            dve.wait_ge(ld_i, 16 * 8)
            for o, i in ((dst_f, dst_i), (src_f, src_i), (same_f, prev_i), (near_f, next_i)):
                link(dve.tensor_copy(o[:, :, :], i[:, :, :]))
            link(dve.tensor_copy(edge2[:, :], edge2_i[:, :]))
            link(dve.tensor_tensor(same_f[:, :, :], same_f[:, :, :], dst_f[:, :, :], ALU.is_equal))
            link(dve.tensor_tensor(near_f[:, :, :], near_f[:, :, :], dst_f[:, :, :], ALU.is_equal))
            link(dve.tensor_scalar(forget_f[:, :, :], same_f[:, :, :], -LOW, LOW, ALU.mult, ALU.add))
            dve.scalar_tensor_tensor(last_f[:, :, :], near_f[:, :, :], FAR, dst_f[:, :, :], ALU.mult, ALU.add).then_inc(k_flags, 1)
            dve.wait_ge(ld_w, 16 * N_LOADS)

            def center(o, i, p0, p1):
                link(dve.tensor_reduce(row_mean[p0:p1, 0:1], i, AX.X, ALU.add))
                link(dve.tensor_scalar(row_mean[p0:p1, 1:2], row_mean[p0:p1, 0:1], -1.0 / D, None, ALU.mult))
                link(dve.tensor_scalar(o, i, row_mean[p0:p1, 1:2], None, ALU.add))

            center(w_out_a[:, 0:D], w_raw[:, 0, :], 0, 128)
            link(dve.tensor_copy(w_out_b[:, D:D2], w_out_a[:, 0:D]))
            link(dve.memset(ones2[0:D, 0:1], 1.0))
            link(dve.memset(ones2[D:D2, 1:2], 1.0))
            dve.wait_ge(k_tr, 1)
            center(w_l1[0:D, 0:D], bank[3][0:D, 0:D], 0, D)
            link(dve.tensor_tensor(w_xi[0:D, :], w_xi[0:D, :], w_xj[0:D, :], ALU.subtract))
            link(dve.tensor_scalar(row_mean[:, 2:3], col_gamma[:, :], STD_EPS_INV, 1.0, ALU.mult, ALU.add))
            for h in range(2):
                a, b = h * D, (h + 1) * D
                center(center2[a:b, a:b], ident[a:b, a:b], a, b)
                link(dve.tensor_tensor(w_raw[a:b, 3, :], w_raw[a:b, 2, :], ident[a:b, a:b], ALU.add))
                center(w_l3[a:b, a:b], w_raw[a:b, 3, :], a, b)
                link(dve.tensor_scalar(w_gamma[a:b, a:b], center2[a:b, a:b], col_gamma[a:b, :], None, ALU.mult))
                link(dve.tensor_scalar(w_l2_dense[a:b, a:b], center2[a:b, a:b], row_mean[a:b, 2:3], None, ALU.mult))
            for l in range(4):
                center(bias[l][:, 0, :], bias_raw[:, l, :], 0, 128)
                for r in range(1, 8):
                    link(dve.tensor_copy(bias[l][:, r, :], bias[l][:, 0, :]))
            for k, o in enumerate((dst_col, src_col, last_col)):
                link(dve.tensor_copy(o[:, :], bank[k][0:P, 0:NT]))
            dve.engine_nop().then_inc(k_idx, 1)
            dve.engine_nop().then_inc(k_ready, 1)

            def norm(o_var, i_sq, o_inv, i_std, o_new, u, squared, summed, stded, inverted, normed, k):
                dve.wait_ge(squared, k)
                dve.tensor_reduce(o_var, i_sq, AX.X, ALU.add).then_inc(summed, 1)
                dve.wait_ge(stded, k)
                dve.reciprocal(o_inv, i_std).then_inc(inverted, 1)
                dve.wait_ge(inverted, k)
                width = u.shape[1]
                dve.tensor_tensor(o_new, u, o_inv.unsqueeze(2).to_broadcast([P, width, D]), ALU.mult).then_inc(normed, 1)

            def dense(n):
                def norm_d(k, o_new):
                    norm(d_var[:, :], d_sq[:, :, :], d_inv[:, :], d_std[:, :], o_new, d_u[:, :, :],
                         d_sqs, d_vs, d_sd, d_iv, d_xs, 4 * n + k)

                def biased(a, l):
                    dve.tensor_tensor(d_u[:, :, :], a, bias[l][0:P, :, :], ALU.add).then_inc(d_us, 1)

                def from_psum(k, l):
                    dve.wait_ge(d_mm, 3 * n + k)
                    biased(d_bank[0][0:P, :].rearrange("p (r d) -> p r d", d=D), l)

                yield
                dve.wait_ge(d_hm, n + 1)
                dve.tensor_scalar(d_hid[1][:, :], d_bank[2][:, 0:CE], col_ub1[:, :], 0.0, ALU.add, ALU.max).then_inc(d_r1, 1)
                yield
                from_psum(1, 0)
                yield
                norm_d(1, d_x[:, :, :])
                dve.wait_ge(d_xs, 4 * n + 1)
                biased(d_x[:, :, :], 1)
                yield
                norm_d(2, d_x[:, :, :])
                yield
                yield
                from_psum(2, 2)
                yield
                norm_d(3, d_x[:, :, :])
                yield
                yield
                from_psum(3, 3)
                yield
                again(dve, d_store, 32, n)
                norm_d(4, d_out[:, :, :])

            def bias_rows(l, t, c):
                y = L[l]
                width = CT if l == 3 else 2 * CT
                dve.wait_ge(prod[c], y.n0 + t + 1)
                dve.tensor_tensor(e_u[c][:, 0:width, :], e_bank[c][0][0:P, 0:width * D].rearrange("p (r d) -> p r d", d=D),
                                  bias[l][0:P, 0:width, :], ALU.add).then_inc(biased[c], 1)

            def tail(l, t, c):
                y = L[l]
                width = CT if l == 3 else 2 * CT
                again(dve, y.stored[c], 16 * CT if l == 3 else 32, t)
                norm(e_var[c][:, 0:width], e_sq[c][:, 0:width, :], e_inv[c][:, 0:width], e_std[c][:, 0:width],
                     e_new[c][:, 0:width, :], e_u[c][:, 0:width, :], sq[c], summed[c], std[c], inv[c], new[c], y.n0 + t + 1)

            def scan(l, t, c, o, i, before, rows, op0, op1, last):
                y = L[l]
                dve.wait_ge(y.flag[c], 16 * t + 16)
                if c == 1:
                    dve.wait_ge(y.scan[0], t + 1)
                else:
                    again(dve, y.scan[1], 1, t)
                ins = dve.tensor_tensor_scan(o[0:rows, :], e_mask[c][0:rows, :], i, before[0:rows, CE - 1:CE], op0, op1)
                if last:
                    ins.then_inc(y.scan[c], 1)

            def layer0(t, c):
                dve.wait_ge(L[0].tr[c], t + 1)
                dve.tensor_copy(e_srcT[c][0:DE, :], e_bank[c][1][0:DE, 0:CE]).then_inc(attr_T[c], 1)
                yield
                yield
                dve.wait_ge(msg_sb[c], t + 1)
                scan(0, t, c, e_agg[c], e_msg[c][:, :], e_agg[1 - c], D, ALU.mult, ALU.add, True)
                yield
                dve.wait_ge(upd_hid[c], t + 1)
                dve.tensor_scalar(e_hidS[c][:, :], e_bank[c][1][:, 0:CE], col_ub1[:, :], 0.0, ALU.add, ALU.max).then_inc(upd_reluS[c], 1)
                yield
                bias_rows(0, t, c)
                yield
                tail(0, t, c)

            def layer1(t, c):
                dve.wait_ge(L[1].tr[c], t + 1)
                scan(1, t, c, e_agg[c], e_bank[c][1][0:D, 0:CE], e_agg[1 - c], D, ALU.mult, ALU.add, True)
                yield
                bias_rows(1, t, c)
                yield
                tail(1, t, c)

            def layer2(t, c):
                dve.wait_ge(L[2].tr[c], t + 1)
                scan(2, t, c, e_deg[c], ones_row[:, :], e_deg[1 - c], 1, ALU.mult, ALU.add, False)
                scan(2, t, c, e_agg[c], e_bank[c][1][:, 0:CE], e_agg[1 - c], D2, ALU.mult, ALU.add, True)
                yield
                m = e_small[c]
                step = stepper(dve, stat[c], STAT_STEPS, t)
                step(dve.tensor_reduce(m[:, 8, :], e_rows[c][:, :, 0:D], AX.X, ALU.add))
                dve.wait_ge(own_sq[c], t + 1)
                step(dve.tensor_reduce(m[:, 9, :], e_u[c][:, 0:CT, :], AX.X, ALU.add))
                dve.wait_ge(sums[c], t + 1)
                got = e_bank[c][1][0:P, 0:2 * CT].rearrange("p (q k) -> p q k", k=2)
                step(dve.tensor_tensor(m[:, 2, :], got[:, :, 0], m[:, 8, :], ALU.add))
                step(dve.tensor_tensor(m[:, 3, :], got[:, :, 1], m[:, 9, :], ALU.add))
                step(dve.tensor_scalar(m[:, 0, :], e_bank[c][1][0:P, 2 * CT:3 * CT], float(D), float(D), ALU.mult, ALU.add))
                step(dve.reciprocal(m[:, 1, :], m[:, 0, :]))
                step(dve.tensor_tensor(m[:, 4, :], m[:, 2, :], m[:, 1, :], ALU.mult))
                step(dve.tensor_copy(e_mean2[c][:, :, 0], m[:, 4, :]))
                step(dve.tensor_tensor(m[:, 5, :], m[:, 0, :], m[:, 4, :], ALU.mult))
                step(dve.tensor_tensor(m[:, 5, :], m[:, 5, :], m[:, 4, :], ALU.mult))
                step(dve.tensor_tensor(m[:, 6, :], m[:, 3, :], m[:, 5, :], ALU.subtract))
                step(dve.tensor_scalar(m[:, 7, :], m[:, 0, :], -1.0, None, ALU.add))
                step(dve.reciprocal(m[:, 7, :], m[:, 7, :]))
                step(dve.tensor_tensor(m[:, 6, :], m[:, 6, :], m[:, 7, :], ALU.mult))
                dve.tensor_scalar(m[:, 6, :], m[:, 6, :], 0.0, None, ALU.max).then_inc(var_ok[c], 1)
                yield
                dve.wait_ge(raw_std[c], t + 1)
                step(dve.tensor_scalar(m[:, 10, :], m[:, 10, :], EPS, None, ALU.add))
                step(dve.reciprocal(e_rstd2[c][:, :, 0], m[:, 10, :]))
                rows = e_rows[c][:, :, :].rearrange("p q (k d) -> p (q k) d", k=2)
                wide = lambda a: a[:, :, :].rearrange("p q k -> p (q k)").unsqueeze(2).to_broadcast([P, 2 * CT, D])
                step(dve.tensor_tensor(e_sq[c][:, :, :], rows, wide(e_mean2[c]), ALU.subtract))
                dve.tensor_tensor(e_sq[c][:, :, :], e_sq[c][:, :, :], wide(e_rstd2[c]), ALU.mult).then_inc(scaled[c], 1)
                yield
                yield
                bias_rows(2, t, c)
                yield
                tail(2, t, c)

            def layer3(t, c):
                dve.wait_ge(L[3].tr[c], t + 1)
                dve.tensor_copy(e_srcT[c][0:D, :], e_bank[c][1][0:D, 0:CE]).then_inc(srcT3[c], 1)
                yield
                dve.wait_ge(vz[c], t + 1)
                scan(3, t, c, e_agg[c], e_bank[c][1][0:D, 0:CE], e_agg[1 - c], D, ALU.add, ALU.max, True)
                dve.wait_ge(L[3].scan[c], t + 1)
                dve.tensor_tensor(e_msg[c][:, :], e_bank[c][0][0:D, 0:CE], e_agg[c][0:D, :], ALU.add).then_inc(z_in[c], 1)
                yield
                bias_rows(3, t, c)
                yield
                tail(3, t, c)

            def know_sources(t):
                for c in range(2):
                    dve.wait_ge(slot_got[c], 16 * CT * t + 16 * CT)
                    step = stepper(dve, slot_fix[c], 2, t)
                    step(dve.tensor_scalar(e_fix[c][:, :], tile_cols(edge2, t, c), 2.0, None, ALU.add))
                    step(dve.scalar_tensor_tensor(e_fix[c][:, :], e_slot[c][:, :], 0.0, e_fix[c][:, :], ALU.is_lt, ALU.mult))
                    dve.tensor_tensor(tile_cols(source_row, t, c), e_slot[c][:, :], e_fix[c][:, :], ALU.add).then_inc(src_known[c], 1)

            phases(dve, dense, (layer0, layer1, layer2, layer3), know_sources)


_INS = ['x', 'src', 'dst', 'edge_attr_32', 'L0_gnn_mW1', 'L0_gnn_mb1', 'L0_gnn_mW2', 'L0_gnn_mb2', 'L0_gnn_uW1',
        'L0_gnn_ub1', 'L0_gnn_uW2', 'L0_gnn_ub2', 'L1_gnn_W', 'L1_gnn_b', 'L2_gnn_gamma', 'L2_gnn_beta',
        'L3_gnn_W_edge', 'L3_gnn_b_edge', 'L3_gnn_W_res', 'L3_gnn_b_res']


def kernel(**inputs):
    import numpy as _np
    import concourse.bacc as _bacc
    from concourse import mybir as _mybir
    from concourse.bass_utils import run_bass_kernel_spmd as _run

    nc = _bacc.Bacc("TRN2", target_bir_lowering=False, num_devices=1)
    arrays, args = {}, []
    for name in _INS:
        a = _np.ascontiguousarray(inputs[name])
        arrays[f"in_{name}_dram"] = a
        args.append(nc.dram_tensor(f"in_{name}_dram", a.shape, _mybir.dt.from_np(a.dtype), kind="ExternalInput").ap())
    args.append(nc.dram_tensor("out_dram", inputs['x'].shape, _mybir.dt.float32, kind="ExternalOutput").ap())
    build_gnn(nc, *args)
    r = _run(nc, [arrays], core_ids=[0])
    return r.results[0]["out_dram"]
```

```python
def build_gnn(nc, x, src, dst, edge_attr, mW1, mb1, mW2, mb2, uW1, ub1, uW2, ub2,
              W1, b1, gamma, beta, W_edge, b_edge, W_res, b_res, out):
    import concourse.bass as bass
    from concourse import mybir
    from contextlib import ExitStack

    f32 = mybir.dt.float32
    i32 = mybir.dt.int32
    ALU = mybir.AluOpType
    ACT = mybir.ActivationFunctionType
    AX = mybir.AxisListType

    N, D = x.shape
    E, DE = edge_attr.shape
    HID = mW1.shape[1]
    P = 125
    D2 = 2 * D
    CT = 4
    CE = CT * P
    NT = E // P
    STEPS = E // (2 * CE)
    R = 8
    BLOCKS = N // (P * R)
    HALF = NT // 2
    PA = 112
    EPS = 1e-5
    STD_EPS_INV = 1.0 / EPS
    FAR = 1048576.0
    N_LOADS = 23
    STAT_STEPS = 18
    LOW = -3.0e38
    assert BLOCKS == 4 * STEPS and NT == 2 * HALF and D2 == 128 and HID == 128

    tables = [nc.dram_tensor(f"edge_rows_{l}", (E, D2), f32, kind="Internal").ap() for l in range(3)]
    slot_table = nc.dram_tensor("slot_table", (N, 1), f32, kind="Internal").ap()
    same_row = nc.dram_tensor("same_row", (1, E), f32, kind="Internal").ap()
    forget_row = nc.dram_tensor("forget_row", (1, E), f32, kind="Internal").ap()
    gather_view = [t.rearrange("e (k d) -> (e k) d", k=2) for t in tables]

    ctx = ExitStack()
    with ctx:
        def sb(name, shape, dt=f32):
            return ctx.enter_context(nc.sbuf_tensor(name, shape, dt))

        def sem(name):
            return ctx.enter_context(nc.semaphore(name))

        ident = sb("ident", [128, 128])
        ones_row = sb("ones_row", [1, CE])
        ones2 = sb("ones2", [128, 2])
        center2 = sb("center2", [128, 128])
        w_upd_top = sb("w_upd_top", [128, 128])
        w_upd_bot = sb("w_upd_bot", [128, 128])
        w_upd_agg = sb("w_upd_agg", [128, 128])
        w_out_a = sb("w_out_a", [128, 128])
        w_out_b = sb("w_out_b", [128, 128])
        w_msg_x = sb("w_msg_x", [128, 128])
        w_msg_e = sb("w_msg_e", [128, 128])
        w_msg_2 = sb("w_msg_2", [128, D])
        w_l1 = sb("w_l1", [128, 128])
        w_gamma = sb("w_gamma", [128, 128])
        w_l2_dense = sb("w_l2_dense", [128, 128])
        w_l3 = sb("w_l3", [128, 128])
        w_xi = sb("w_xi", [128, D])
        w_xj = sb("w_xj", [128, D])
        w_raw = sb("w_raw", [128, 4, D])
        row_mean = sb("row_mean", [128, 8])
        bias = [sb(f"bias_{l}", [128, 8, D]) for l in range(4)]
        bias_raw = sb("bias_raw", [128, 4, D])
        col_mb1 = sb("col_mb1", [128, 1])
        col_ub1 = sb("col_ub1", [128, 1])
        col_mb2 = sb("col_mb2", [D, 1])
        col_be = sb("col_be", [D, 1])
        col_gamma = sb("col_gamma", [128, 1])
        col_eps = sb("col_eps", [128, 1])
        col_zero = sb("col_zero", [128, 1])
        minus_one = sb("minus_one", [P, N // P])

        dst_i = sb("dst_i", [HALF, 2, P], i32)
        src_i = sb("src_i", [HALF, 2, P], i32)
        prev_i = sb("prev_i", [HALF, 2, P], i32)
        next_i = sb("next_i", [HALF, 2, P], i32)
        dst_f = sb("dst_f", [HALF, 2, P])
        src_f = sb("src_f", [HALF, 2, P])
        near_f = sb("near_f", [HALF, 2, P])
        last_f = sb("last_f", [HALF, 2, P])
        same_f = sb("same_f", [HALF, 2, P])
        forget_f = sb("forget_f", [HALF, 2, P])
        dst_col = sb("dst_col", [P, NT], i32)
        src_col = sb("src_col", [P, NT], i32)
        last_col = sb("last_col", [P, NT], i32)
        source_row = sb("source_row", [P, NT], i32)
        edge2_i = sb("edge2_i", [P, NT], i32)
        edge2 = sb("edge2", [P, NT])

        d_rows = sb("d_rows", [P, R * D])
        d_rowsT = [sb(f"d_rowsT{h}", [128, CE]) for h in range(2)]
        d_hid = [sb(f"d_hid{h}", [128, CE]) for h in range(2)]
        d_u = [sb(f"d_u{h}", [P, R, D]) for h in range(2)]
        d_sq = [sb(f"d_sq{h}", [P, R, D]) for h in range(2)]
        d_x = [sb(f"d_x{l}", [P, R, D]) for l in range(3)]
        d_out = sb("d_out", [P, R, D])
        d_var = [sb(f"d_var{h}", [P, R]) for h in range(2)]
        d_std = [sb(f"d_std{h}", [P, R]) for h in range(2)]
        d_inv = [sb(f"d_inv{h}", [P, R]) for h in range(2)]

        def two(name, shape, dt=f32):
            return [sb(f"{name}{c}", shape, dt) for c in range(2)]

        e_idx = two("e_idx", [P, 3 * CT], i32)
        e_val = two("e_val", [P, CT])
        e_slot = two("e_slot", [P, CT])
        e_fix = two("e_fix", [P, CT])
        e_rows = two("e_rows", [P, CT, D2])
        e_src = two("e_src", [P, CT, D2])
        e_attr = two("e_attr", [P, CT, DE])
        e_mask = two("e_mask", [128, CE])
        e_rowsT = two("e_rowsT", [128, CE])
        e_srcT = two("e_srcT", [128, CE])
        e_hid = two("e_hid", [128, CE])
        e_hidS = two("e_hidS", [128, CE])
        e_msg = two("e_msg", [D, CE])
        e_agg = two("e_agg", [128, CE])
        e_deg = two("e_deg", [1, CE])
        e_u = two("e_u", [P, 2 * CT, D])
        e_sq = two("e_sq", [P, 2 * CT, D])
        e_new = two("e_new", [P, 2 * CT, D])
        e_var = two("e_var", [P, 2 * CT])
        e_std = two("e_std", [P, 2 * CT])
        e_inv = two("e_inv", [P, 2 * CT])
        e_small = two("e_small", [P, 12, CT])
        e_mean2 = two("e_mean2", [P, CT, 2])
        e_rstd2 = two("e_rstd2", [P, CT, 2])

        bank = [ctx.enter_context(nc.psum_tensor(f"bank{i}", [128, 512], f32)) for i in range(8)]
        d_bank = bank[0:3]
        d_bank_b = bank[7]
        e_bank = [bank[3:5], bank[5:7]]

        k_zero = sem("k_zero")
        k_ident = sem("k_ident")
        ld_w = sem("ld_w")
        ld_i = sem("ld_i")
        k_dve = sem("k_dve")
        k_flags = sem("k_flags")
        k_tr = sem("k_tr")
        k_idx = sem("k_idx")
        k_ready = sem("k_ready")
        flags_out = sem("flags_out")
        slots_clear = sem("slots_clear")
        out_done = sem("out_done")

        def pair(name):
            return [sem(f"{name}_{c}") for c in range(2)]

        slots_set = pair("slots_set")
        slot_idx = pair("slot_idx")
        slot_got = pair("slot_got")
        slot_fix = pair("slot_fix")
        src_known = pair("src_known")

        d_load, d_hm, d_relu, d_store = [
            sem(f"dense_{n}") for n in ("loaded", "hidden", "relu", "stored")]
        d_tr, d_ev, d_mm, d_us, d_sqs, d_vs, d_sd, d_iv, d_xs = [
            pair(f"dense_{n}") for n in ("transposed", "evacuated", "product", "biased", "squared", "summed", "std",
                                         "inverse", "normed")]

        class Layer:
            pass

        L = [Layer() for _ in range(4)]
        tr = pair("tr")
        scanned = pair("scanned")
        rowsT = pair("rowsT")
        prod = pair("prod")
        biased = pair("biased")
        sq = pair("sq")
        summed = pair("summed")
        std = pair("std")
        inv = pair("inv")
        new = pair("new")
        for l, y in enumerate(L):
            y.n0 = l * STEPS
            y.r0 = STEPS if l == 3 else 0
            y.idx = pair(f"idx{l}")
            y.got = pair(f"got{l}")
            y.flag = pair(f"flag{l}")
            y.stored = pair(f"stored{l}")
            if l == 0:
                y.attr = pair("attr0")
            else:
                y.rows = pair(f"rows{l}")
        attr_T = pair("attr_T")
        msg_hid = pair("msg_hid"); msg_relu = pair("msg_relu")
        msg_out = pair("msg_out"); msg_sb = pair("msg_sb")
        upd_hid = pair("upd_hid"); upd_relu = pair("upd_relu")
        src_sq = pair("src_sq"); own_sq = pair("own_sq")
        sums = pair("sums"); stat = pair("stat"); raw_std = pair("raw_std"); var_ok = pair("var_ok")
        scaled = pair("scaled"); scaled_tr = pair("scaled_tr"); scaled_T = pair("scaled_T")
        last_idx = pair("last_idx")
        srcT3 = pair("srcT3"); vz = pair("vz"); z_in = pair("z_in"); z_relu = pair("z_relu")

        block = ctx.enter_context(nc.Block())

        def in_turn(*chains):
            live = list(chains)
            while live:
                for chain in list(live):
                    if next(chain, "end") == "end":
                        live.remove(chain)

        base = {0: 0, "slots": STEPS, 1: 2 * STEPS, 2: 3 * STEPS}

        def phases(eng, dense, layers, slots):
            a, b = dense

            def step0(t):
                n = base[0] + t
                if isinstance(t, int):
                    in_turn(layers[0](t, 0), layers[0](t, 1), a(n))
                else:
                    in_turn(layers[0](t, 0), layers[0](t, 1), a(n), b(n - 1))

            def step_slots(t):
                n = base["slots"] + t
                if slots is not None:
                    slots(t)
                in_turn(a(n), b(n - 1))

            def step1(t):
                n = base[1] + t
                in_turn(layers[1](t, 0), layers[1](t, 1), a(n), b(n - 1))

            def step2(t):
                n = base[2] + t
                in_turn(layers[2](t, 0), layers[2](t, 1), a(n), b(n - 1))

            def step3(t):
                if isinstance(t, int):
                    in_turn(layers[3](t, 0), layers[3](t, 1), b(BLOCKS - 1))
                else:
                    in_turn(layers[3](t, 0), layers[3](t, 1))

            for step in (step0, step_slots, step1, step2, step3):
                step(0)
                with eng.Fori(1, STEPS) as t:
                    step(t)

        def again(eng, s, per, t):
            if not isinstance(t, int) or t > 0:
                eng.wait_ge(s, per * t)

        def stepper(eng, s, per, t):
            done = [0]

            def step(ins):
                done[0] += 1
                ins.then_inc(s, 1)
                eng.wait_ge(s, per * t + done[0])
            return step

        def rows_dma(eng, o, i, s):
            eng.dma_start(o[0:PA], i[0:PA]).then_inc(s, 16)
            eng.dma_start(o[PA:P], i[PA:P]).then_inc(s, 16)

        def dense_rows(a, n):
            return a[bass.ds(n * (P * R), P * R), :].rearrange("(p r) d -> p r d", r=R)

        def edge_cols(a, t, c):
            return a[0:1, bass.ds(t * (2 * CE) + c * CE, CE)]

        def edge_rows(a, t, c):
            return a[bass.ds(t * (2 * CE) + c * CE, CE), :].rearrange("(j p) d -> p j d", p=P)

        def tile_cols(a, t, c):
            return a[:, bass.ds(t * (2 * CT) + c * CT, CT)]

        @block.sync
        def _(sp):
            def halves(a, lo):
                return a[lo:lo + 2 * HALF * P].rearrange("(g t p) -> t g p", g=2, p=P)

            sp.wait_ge(k_zero, 1)
            sp.dma_start(dst_i[:, :, :], halves(dst, 0)).then_inc(ld_i, 16)
            sp.dma_start(src_i[:, :, :], halves(src, 0)).then_inc(ld_i, 16)
            one = dst[0:P - 1].rearrange("(a p) -> a p", a=1)
            sp.dma_start(prev_i[0:1, 0, 1:P], one).then_inc(ld_i, 16)
            sp.dma_start(prev_i[1:HALF, 0, :], dst[P - 1:HALF * P - 1].rearrange("(t p) -> t p", p=P)).then_inc(ld_i, 16)
            sp.dma_start(prev_i[:, 1, :], dst[HALF * P - 1:E - 1].rearrange("(t p) -> t p", p=P)).then_inc(ld_i, 16)
            sp.dma_start(next_i[:, 0, :], dst[1:HALF * P + 1].rearrange("(t p) -> t p", p=P)).then_inc(ld_i, 16)
            sp.dma_start(next_i[0:HALF - 1, 1, :], dst[HALF * P + 1:E - P + 1].rearrange("(t p) -> t p", p=P)).then_inc(ld_i, 16)
            one = dst[E - P + 1:E].rearrange("(a p) -> a p", a=1)
            sp.dma_start(next_i[HALF - 1:HALF, 1, 0:P - 1], one).then_inc(ld_i, 16)
            sp.dma_start(slot_table.rearrange("(p k) o -> p (k o)", p=P), minus_one[:, :]).then_inc(slots_clear, 16)
            col = lambda a: a.rearrange("(p o) -> p o", o=1)
            for o, i in (
                (w_upd_top[0:D, :], uW1[0:D, :]), (w_upd_bot[D:D2, :], uW1[0:D, :]),
                (w_upd_agg[0:D, :], uW1[D:D2, :]),
                (w_msg_x[0:D, :], mW1[D:D2, :]), (w_msg_x[D:D2, :], mW1[0:D, :]),
                (w_msg_e[0:DE, :], mW1[D2:D2 + DE, :]), (w_msg_2[:, :], mW2),
                (w_raw[:, 0, :], uW2), (w_raw[0:D, 1, :], W1),
                (w_raw[0:D, 2, :], W_res), (w_raw[D:D2, 2, :], W_res),
                (w_xi[0:D, :], W_edge[0:D, :]), (w_xj[0:D, :], W_edge[D:D2, :]),
                (col_mb1[:, :], col(mb1)), (col_ub1[:, :], col(ub1)), (col_mb2[:, :], col(mb2)),
                (col_be[:, :], col(b_edge)), (col_gamma[0:D, :], col(gamma)), (col_gamma[D:D2, :], col(gamma)),
                (bias_raw[:, 0, :], ub2.partition_broadcast(128)), (bias_raw[:, 1, :], b1.partition_broadcast(128)),
                (bias_raw[:, 2, :], beta.partition_broadcast(128)), (bias_raw[:, 3, :], b_res.partition_broadcast(128)),
            ):
                sp.dma_start(o, i).then_inc(ld_w, 16)
            sp.wait_ge(k_flags, 1)
            sp.dma_start(halves(same_row[0, :], 0), same_f[:, :, :]).then_inc(flags_out, 16)
            sp.dma_start(halves(forget_row[0, :], 0), forget_f[:, :, :]).then_inc(flags_out, 16)
            sp.wait_ge(flags_out, 32)

            def load_dense(n):
                again(sp, d_tr[0], 1, n)
                rows_dma(sp, d_rows[:, :].rearrange("p (r d) -> p r d", r=R), dense_rows(x, n), d_load)

            def store_dense(n):
                sp.wait_ge(d_xs[1], 2 * n + 2)
                rows_dma(sp, dense_rows(out, n), d_out, d_store)

            def load(l, t, c):
                y = L[l]
                again(sp, scanned[c], 1, y.n0 + t)
                flag = forget_row if l == 3 else same_row
                sp.dma_start(e_mask[c][:, :], edge_cols(flag, t, c)[0, :].partition_broadcast(128)).then_inc(y.flag[c], 16)
                if l == 0:
                    again(sp, tr[c], 1, t)
                    rows_dma(sp, e_attr[c], edge_rows(edge_attr, t, c), y.attr[c])
                else:
                    if l == 1:
                        again(sp, biased[c], 1, y.n0 + t)
                    elif l == 2:
                        again(sp, scaled[c], 1, t)
                    else:
                        again(sp, tr[c], 1, y.n0 + t)
                    rows_dma(sp, e_rows[c], edge_rows(tables[l - 1], t, c), y.rows[c])

            def store(l, t, c):
                y = L[l]
                sp.wait_ge(new[c], y.n0 + t + 1)
                rows = e_new[c][:, :, :].rearrange("p (j k) d -> p j (k d)", k=2)
                rows_dma(sp, edge_rows(tables[l], t, c), rows, y.stored[c])

            def step(l, t):
                for c in range(2):
                    load(l, t, c)
                load_dense(base[l] + t)
                if not isinstance(t, int) or t > 0:
                    for c in range(2):
                        store(l, t - 1, c)
                if l > 0 or not isinstance(t, int):
                    store_dense(base[l] + t - 2)

            def after_layer(l):
                for c in range(2):
                    store(l, STEPS - 1, c)
                for c in range(2):
                    sp.wait_ge(L[l].stored[c], 32 * STEPS)

            step(0, 0)
            step(0, 1)
            with sp.Fori(2, STEPS) as t:
                step(0, t)
            after_layer(0)
            with sp.Fori(0, STEPS) as t:
                load_dense(base["slots"] + t)
                store_dense(base["slots"] + t - 2)
            for l in (1, 2):
                step(l, 0)
                with sp.Fori(1, STEPS) as t:
                    step(l, t)
                after_layer(l)
            for c in range(2):
                load(3, 0, c)
            store_dense(BLOCKS - 2)
            store_dense(BLOCKS - 1)
            with sp.Fori(1, STEPS) as t:
                for c in range(2):
                    load(3, t, c)
            sp.wait_ge(d_store, 32 * BLOCKS)
            for c in range(2):
                sp.wait_ge(slots_set[c], 16 * CT * STEPS)
                sp.wait_ge(L[3].stored[c], 16 * CT * STEPS)
            sp.wait_ge(slots_clear, 16)

        @block.gpsimd
        def _(pool):
            pool.memset(prev_i[:, :, :], -1)
            pool.memset(next_i[:, :, :], -1)
            pool.memset(minus_one[:, :], -1.0)
            pool.memset(ones_row[:, :], 1.0)
            pool.memset(ones2[:, :], 0.0)
            pool.memset(col_eps[:, :], EPS)
            for w in (w_upd_top, w_upd_bot, w_upd_agg, w_out_a, w_out_b, w_msg_e, w_l1, w_l2_dense, w_l3,
                      w_gamma, center2, w_xi, w_xj):
                pool.memset(w[:, :], 0.0)
            for c in range(2):
                pool.memset(e_agg[c][:, :], 0.0)
                pool.memset(e_srcT[c][:, :], 0.0)
                pool.memset(e_hid[c][:, :], 0.0)
                pool.memset(e_deg[c][:, :], 0.0)
                pool.memset(e_mean2[c][:, :, :], 0.0)
                pool.memset(e_rstd2[c][:, :, :], STD_EPS_INV)
            pool.memset(ident[:, :], 0.0).then_inc(k_zero, 1)
            pool.iota(edge2_i[:, :], pattern=[[2 * P, NT]], base=0, channel_multiplier=2).then_inc(k_ident, 1)
            pool.wait_ge(k_zero, 1)
            pool.affine_select(out=ident[:, :], in_=ident[:, :], compare_op=ALU.not_equal, fill=1.0, base=0,
                               pattern=[[-1, 128]], channel_multiplier=1).then_inc(k_ident, 1)
            pool.wait_ge(k_idx, 1)

            def copy_idx(c, t, s, parts):
                for k, table in enumerate(parts):
                    last = pool.tensor_copy(e_idx[c][:, k * CT:(k + 1) * CT], tile_cols(table, t, c))
                last.then_inc(s, 1)
                pool.wait_ge(s, t + 1)
                pool.nop(nofuse=True)

            def gather(o, table, c, k, s):
                pool.indirect_dma_start(out=o, out_offset=None, in_=table, in_offset=bass.IndirectOffsetOnAxis(
                    ap=e_idx[c][:, k:k + 1], axis=0)).then_inc(s, 16)

            def scatter(table, i, c, k, s):
                pool.indirect_dma_start(out=table, out_offset=bass.IndirectOffsetOnAxis(
                    ap=e_idx[c][:, k:k + 1], axis=0), in_=i, in_offset=None,
                    bounds_check=N - 1, oob_is_err=False).then_inc(s, 16)

            def layer0(t):
                for c in range(2):
                    again(pool, tr[c], 1, t)
                    again(pool, slots_set[c], 16 * CT, t)
                    pool.tensor_copy(e_val[c][:, :], tile_cols(edge2, t, c))
                    copy_idx(c, t, L[0].idx[c], (dst_col, src_col, last_col))
                    for j in range(CT):
                        gather(e_rows[c][:, j, 0:D], x, c, j, L[0].got[c])
                        gather(e_rows[c][:, j, D:D2], x, c, CT + j, L[0].got[c])
                    for j in range(CT):
                        scatter(slot_table, e_val[c][:, j:j + 1], c, 2 * CT + j, slots_set[c])

            def slots(t):
                for c in range(2):
                    again(pool, src_known[c], 1, t)
                    copy_idx(c, t, slot_idx[c], (src_col,))
                    for j in range(CT):
                        gather(e_slot[c][:, j:j + 1], slot_table, c, j, slot_got[c])

            def sources(l, t):
                for c in range(2):
                    again(pool, tr[c], 1, L[l].n0 + t)
                    copy_idx(c, t, L[l].idx[c], (source_row,))
                    for j in range(CT):
                        gather(e_src[c][:, j, 0:D], gather_view[l - 1], c, j, L[l].got[c])

            def results(t):
                for c in range(2):
                    again(pool, L[3].stored[c], 16 * CT, t)
                    pool.tensor_copy(e_idx[c][:, CT:2 * CT], tile_cols(last_col, t, c)).then_inc(last_idx[c], 1)
                    pool.wait_ge(last_idx[c], t + 1)
                    pool.wait_ge(new[c], L[3].n0 + t + 1)
                    pool.nop(nofuse=True)
                    for j in range(CT):
                        scatter(out, e_new[c][:, j, :], c, CT + j, L[3].stored[c])

            pool.wait_ge(slots_clear, 16)
            layer0(0)
            with pool.Fori(1, STEPS) as t:
                layer0(t)
            for c in range(2):
                pool.wait_ge(slots_set[c], 16 * CT * STEPS)
            slots(0)
            with pool.Fori(1, STEPS) as t:
                slots(t)
            for c in range(2):
                pool.wait_ge(src_known[c], STEPS)
            for l in (1, 2):
                for c in range(2):
                    pool.wait_ge(L[l - 1].stored[c], 32 * STEPS)
                sources(l, 0)
                with pool.Fori(1, STEPS) as t:
                    sources(l, t)
            for c in range(2):
                pool.wait_ge(L[2].stored[c], 32 * STEPS)
            sources(3, 0)
            sources(3, 1)
            pool.wait_ge(d_store, 32 * BLOCKS)
            results(0)
            with pool.Fori(2, STEPS) as t:
                sources(3, t)
                results(t - 1)
            results(STEPS - 1)

        @block.tensor
        def _(pe):
            pe.wait_ge(k_flags, 1)
            for k, a in enumerate((dst_f, src_f, last_f)):
                for g in range(2):
                    pe.transpose(bank[k][0:P, g * HALF:(g + 1) * HALF], a[:, g, :], ident[0:HALF, 0:HALF])
            pe.wait_ge(ld_w, 16 * N_LOADS)
            pe.transpose(bank[3][0:D, 0:D], w_raw[0:D, 1, :], ident[0:D, 0:D]).then_inc(k_tr, 1)
            pe.wait_ge(k_ready, 1)

            def pair_transposes(o, rows, s):
                for q in range(CT):
                    last = pe.transpose(o[:, q * P:(q + 1) * P], rows(q), ident[0:P, 0:P])
                if s is not None:
                    last.then_inc(s, 1)
                return last

            def products(o, width, terms, s):
                for q in range(CT):
                    for k, (a, w) in enumerate(terms):
                        last = pe.matmul(o[0:P, q * width:(q + 1) * width], a[:, q * P:(q + 1) * P], w,
                                         start=k == 0, stop=k == len(terms) - 1)
                last.then_inc(s, 1)

            def dense_a(n):
                b = d_bank
                pe.wait_ge(d_load, 32 * n + 32)
                again(pe, d_us[0], 2, n)
                pair_transposes(b[0], lambda q: d_rows[:, q * D2:(q + 1) * D2], d_tr[0])
                yield
                pe.wait_ge(d_ev[0], n + 1)
                pe.matmul(b[1][:, 0:CE], w_upd_top[:, :], d_rowsT[0][:, :], start=True, stop=True)
                pe.matmul(b[2][:, 0:CE], w_upd_bot[:, :], d_rowsT[0][:, :], start=True, stop=True).then_inc(d_hm, 1)
                yield
                pe.wait_ge(d_relu, n + 1)
                products(b[0], D2, ((d_hid[0], w_out_a[:, :]), (d_hid[1], w_out_b[:, :]), (d_rowsT[0], center2[:, :])), d_mm[0])

            def dense_b(n):
                for k, w in ((1, w_l2_dense), (2, w_l3)):
                    pe.wait_ge(*((d_xs[0], 2 * n + 2) if k == 1 else (d_xs[1], 2 * n + 1)))
                    if k == 1:
                        again(pe, d_us[1], 2, n)
                    pair_transposes(d_bank_b, lambda q: d_x[k][:, 2 * q:2 * q + 2, :].rearrange("p r d -> p (r d)"), d_tr[1])
                    yield
                    pe.wait_ge(d_ev[1], 2 * n + k)
                    products(d_bank_b, D2, ((d_rowsT[1], w[:, :]),), d_mm[1])
                    yield
                    yield

            def layer0(t, c):
                y, (b0, b1) = L[0], e_bank[c]
                pe.wait_ge(y.got[c], 32 * CT * t + 32 * CT)
                again(pe, biased[c], 1, y.n0 + t)
                pair_transposes(b0, lambda q: e_rows[c][:, q, :], None)
                pe.wait_ge(y.attr[c], 32 * t + 32)
                for q in range(CT):
                    last = pe.transpose(b1[0:DE, q * P:(q + 1) * P], e_attr[c][:, q, :], ident[0:P, 0:P])
                last.then_inc(tr[c], 1)
                yield
                pe.wait_ge(rowsT[c], y.r0 + t + 1)
                pe.wait_ge(attr_T[c], t + 1)
                pe.matmul(b0[:, 0:CE], w_msg_x[:, :], e_rowsT[c][:, :], start=True, stop=False)
                pe.matmul(b0[:, 0:CE], w_msg_e[:, :], e_srcT[c][:, :], start=False, stop=True).then_inc(msg_hid[c], 1)
                yield
                pe.wait_ge(msg_relu[c], t + 1)
                pe.matmul(b1[0:D, 0:CE], w_msg_2[:, :], e_hid[c][:, :], start=True, stop=True).then_inc(msg_out[c], 1)
                yield
                pe.wait_ge(scanned[c], y.n0 + t + 1)
                pe.matmul(b0[:, 0:CE], w_upd_top[:, :], e_rowsT[c][:, :], start=True, stop=False)
                pe.matmul(b0[:, 0:CE], w_upd_agg[:, :], e_agg[c][:, :], start=False, stop=True)
                pe.matmul(b1[:, 0:CE], w_upd_bot[:, :], e_rowsT[c][:, :], start=True, stop=True).then_inc(upd_hid[c], 1)
                yield
                pe.wait_ge(upd_relu[c], t + 1)
                products(b0, D2, ((e_hid[c], w_out_a[:, :]), (e_hidS[c], w_out_b[:, :]), (e_rowsT[c], center2[:, :])), prod[c])

            def transpose_sources(y, b1, c, t, width):
                pe.wait_ge(y.got[c], 16 * CT * t + 16 * CT)
                pe.nop(nofuse=True)
                for q in range(CT):
                    last = pe.transpose(b1[0:width, q * P:(q + 1) * P], e_src[c][:, q, 0:width], ident[0:P, 0:P])
                last.then_inc(tr[c], 1)

            def transpose_rows(y, b0, c, t):
                pe.wait_ge(y.rows[c], 32 * t + 32)
                again(pe, biased[c], 1, y.n0 + t)
                pair_transposes(b0, lambda q: e_rows[c][:, q, :], None)

            def layer1(t, c):
                y, (b0, b1) = L[1], e_bank[c]
                again(pe, scanned[c], 1, y.n0 + t)
                transpose_sources(y, b1, c, t, D)
                yield
                pe.wait_ge(scanned[c], y.n0 + t + 1)
                again(pe, biased[c], 1, y.n0 + t)
                products(b0, D2, ((e_agg[c], w_l1[:, :]),), prod[c])

            def layer2(t, c):
                y, (b0, b1) = L[2], e_bank[c]
                again(pe, scaled_T[c], 1, t)
                pe.wait_ge(src_sq[c], t + 1)
                transpose_sources(y, b1, c, t, D2)
                yield
                pe.wait_ge(scanned[c], y.n0 + t + 1)
                for q in range(CT):
                    pe.matmul(b1[0:P, 2 * q:2 * q + 2], e_agg[c][:, q * P:(q + 1) * P], ones2[:, :], start=True, stop=True)
                for q in range(CT):
                    last = pe.matmul(b1[0:P, 2 * CT + q:2 * CT + q + 1], e_deg[c][0:1, q * P:(q + 1) * P],
                                     ones_row[0:1, 0:1], start=True, stop=True)
                last.then_inc(sums[c], 1)
                yield
                yield
                pe.wait_ge(scaled[c], t + 1)
                pair_transposes(b1, lambda q: e_sq[c][:, 2 * q:2 * q + 2, :].rearrange("p r d -> p (r d)"), scaled_tr[c])
                yield
                pe.wait_ge(scaled_T[c], t + 1)
                again(pe, biased[c], 1, y.n0 + t)
                products(b0, D2, ((e_srcT[c], w_gamma[:, :]),), prod[c])

            def layer3(t, c):
                y, (b0, b1) = L[3], e_bank[c]
                transpose_rows(y, b0, c, t)
                transpose_sources(y, b1, c, t, D)
                yield
                pe.wait_ge(rowsT[c], y.r0 + t + 1)
                pe.wait_ge(srcT3[c], t + 1)
                pe.matmul(b1[0:D, 0:CE], w_xj[:, :], e_srcT[c][:, :], start=True, stop=True)
                pe.matmul(b0[0:D, 0:CE], w_xi[:, :], e_rowsT[c][:, :], start=True, stop=True).then_inc(vz[c], 1)
                yield
                pe.wait_ge(z_relu[c], t + 1)
                products(b0, D, ((e_rowsT[c], w_l3[:, 0:D]), (e_hid[c], center2[:, 0:D])), prod[c])

            phases(pe, (dense_a, dense_b), (layer0, layer1, layer2, layer3), None)

        @block.scalar
        def _(act):
            act.wait_ge(k_ready, 1)

            def norm(o_sq, u, var, o_std, biased, squared, summed, stded, k):
                act.wait_ge(biased, k)
                act.activation(o_sq, u, ACT.Square).then_inc(squared, 1)
                yield
                act.wait_ge(summed, k)
                act.activation(o_std, var, ACT.Sqrt, bias=col_eps[0:P, :], scale=1.0 / D).then_inc(stded, 1)

            def norm_d(h, n, k):
                return norm(d_sq[h][:, :, :], d_u[h][:, :, :], d_var[h][:, :], d_std[h][:, :],
                            d_us[h], d_sqs[h], d_vs[h], d_sd[h], 2 * n + k)

            def evacuate(b, h, k):
                act.wait_ge(d_tr[h], k)
                act.activation(d_rowsT[h][:, :], b[:, 0:CE], ACT.Copy).then_inc(d_ev[h], 1)

            def dense_a(n):
                again(act, d_mm[0], 1, n)
                evacuate(d_bank[0], 0, n + 1)
                yield
                act.wait_ge(d_hm, n + 1)
                for h in range(2):
                    last = act.activation(d_hid[h][:, :], d_bank[1 + h][:, 0:CE], ACT.Relu, bias=col_ub1[:, :])
                last.then_inc(d_relu, 1)
                yield
                yield from norm_d(0, n, 1)
                yield from norm_d(0, n, 2)

            def dense_b(n):
                again(act, d_mm[1], 2, n)
                evacuate(d_bank_b, 1, 2 * n + 1)
                yield
                yield from norm_d(1, n, 1)
                yield
                evacuate(d_bank_b, 1, 2 * n + 2)
                yield
                yield from norm_d(1, n, 2)

            def tail(l, t, c, width):
                y = L[l]
                yield from norm(e_sq[c][:, 0:width, :], e_u[c][:, 0:width, :], e_var[c][:, 0:width], e_std[c][:, 0:width],
                                biased[c], sq[c], summed[c], std[c], y.n0 + t + 1)

            def rows_T(l, t, c):
                act.wait_ge(tr[c], L[l].n0 + t + 1)
                act.activation(e_rowsT[c][:, :], e_bank[c][0][:, 0:CE], ACT.Copy).then_inc(rowsT[c], 1)

            def layer0(t, c):
                rows_T(0, t, c)
                yield
                act.wait_ge(msg_hid[c], t + 1)
                act.activation(e_hid[c][:, :], e_bank[c][0][:, 0:CE], ACT.Relu, bias=col_mb1[:, :]).then_inc(msg_relu[c], 1)
                yield
                act.wait_ge(msg_out[c], t + 1)
                act.activation(e_msg[c][:, :], e_bank[c][1][0:D, 0:CE], ACT.Identity, bias=col_mb2[:, :]).then_inc(msg_sb[c], 1)
                yield
                act.wait_ge(upd_hid[c], t + 1)
                act.activation(e_hid[c][:, :], e_bank[c][0][:, 0:CE], ACT.Relu, bias=col_ub1[:, :])
                act.activation(e_hidS[c][:, :], e_bank[c][1][:, 0:CE], ACT.Relu, bias=col_ub1[:, :]).then_inc(upd_relu[c], 1)
                yield
                yield from tail(0, t, c, 2 * CT)

            def layer1(t, c):
                yield
                yield from tail(1, t, c, 2 * CT)

            def layer2(t, c):
                act.wait_ge(L[2].got[c], 16 * CT * t + 16 * CT)
                act.activation(e_src[c][:, :, D:D2], e_src[c][:, :, 0:D], ACT.Square).then_inc(src_sq[c], 1)
                act.wait_ge(L[2].rows[c], 32 * t + 32)
                act.activation(e_u[c][:, 0:CT, :], e_rows[c][:, :, 0:D], ACT.Square).then_inc(own_sq[c], 1)
                yield
                act.wait_ge(var_ok[c], t + 1)
                act.activation(e_small[c][:, 10, :], e_small[c][:, 6, :], ACT.Sqrt).then_inc(raw_std[c], 1)
                yield
                yield
                act.wait_ge(scaled_tr[c], t + 1)
                act.activation(e_srcT[c][:, :], e_bank[c][1][:, 0:CE], ACT.Copy).then_inc(scaled_T[c], 1)
                yield
                yield from tail(2, t, c, 2 * CT)

            def layer3(t, c):
                rows_T(3, t, c)
                yield
                act.wait_ge(z_in[c], t + 1)
                act.activation(e_hid[c][0:D, :], e_msg[c][:, :], ACT.Relu, bias=col_be[:, :]).then_inc(z_relu[c], 1)
                yield
                yield from tail(3, t, c, CT)

            phases(act, (dense_a, dense_b), (layer0, layer1, layer2, layer3), None)

        @block.vector
        def _(dve):
            link = stepper(dve, k_dve, 0, 0)
            dve.wait_ge(k_ident, 2)
            dve.wait_ge(ld_i, 16 * 8)
            for o, i in ((dst_f, dst_i), (src_f, src_i), (same_f, prev_i), (near_f, next_i)):
                link(dve.tensor_copy(o[:, :, :], i[:, :, :]))
            link(dve.tensor_copy(edge2[:, :], edge2_i[:, :]))
            link(dve.tensor_tensor(same_f[:, :, :], same_f[:, :, :], dst_f[:, :, :], ALU.is_equal))
            link(dve.tensor_tensor(near_f[:, :, :], near_f[:, :, :], dst_f[:, :, :], ALU.is_equal))
            link(dve.tensor_scalar(forget_f[:, :, :], same_f[:, :, :], -LOW, LOW, ALU.mult, ALU.add))
            dve.scalar_tensor_tensor(last_f[:, :, :], near_f[:, :, :], FAR, dst_f[:, :, :], ALU.mult, ALU.add).then_inc(k_flags, 1)
            dve.wait_ge(ld_w, 16 * N_LOADS)

            def center(o, i, p0, p1):
                link(dve.tensor_reduce(row_mean[p0:p1, 0:1], i, AX.X, ALU.add))
                link(dve.tensor_scalar(row_mean[p0:p1, 1:2], row_mean[p0:p1, 0:1], -1.0 / D, None, ALU.mult))
                link(dve.tensor_scalar(o, i, row_mean[p0:p1, 1:2], None, ALU.add))

            center(w_out_a[:, 0:D], w_raw[:, 0, :], 0, 128)
            link(dve.tensor_copy(w_out_b[:, D:D2], w_out_a[:, 0:D]))
            link(dve.memset(ones2[0:D, 0:1], 1.0))
            link(dve.memset(ones2[D:D2, 1:2], 1.0))
            dve.wait_ge(k_tr, 1)
            center(w_l1[0:D, 0:D], bank[3][0:D, 0:D], 0, D)
            link(dve.tensor_tensor(w_xi[0:D, :], w_xi[0:D, :], w_xj[0:D, :], ALU.subtract))
            link(dve.tensor_scalar(row_mean[:, 2:3], col_gamma[:, :], STD_EPS_INV, 1.0, ALU.mult, ALU.add))
            for h in range(2):
                a, b = h * D, (h + 1) * D
                center(center2[a:b, a:b], ident[a:b, a:b], a, b)
                link(dve.tensor_tensor(w_raw[a:b, 3, :], w_raw[a:b, 2, :], ident[a:b, a:b], ALU.add))
                center(w_l3[a:b, a:b], w_raw[a:b, 3, :], a, b)
                link(dve.tensor_scalar(w_gamma[a:b, a:b], center2[a:b, a:b], col_gamma[a:b, :], None, ALU.mult))
                link(dve.tensor_scalar(w_l2_dense[a:b, a:b], center2[a:b, a:b], row_mean[a:b, 2:3], None, ALU.mult))
            for l in range(4):
                center(bias[l][:, 0, :], bias_raw[:, l, :], 0, 128)
                for r in range(1, 8):
                    link(dve.tensor_copy(bias[l][:, r, :], bias[l][:, 0, :]))
            for h in range(2):
                link(dve.tensor_copy(w_l1[D:D + 1, h * D:(h + 1) * D], bias[1][D:D + 1, 0, :]))
                link(dve.memset(e_agg[h][D:D + 1, :], 1.0))
            for k, o in enumerate((dst_col, src_col, last_col)):
                link(dve.tensor_copy(o[:, :], bank[k][0:P, 0:NT]))
            dve.engine_nop().then_inc(k_idx, 1)
            dve.engine_nop().then_inc(k_ready, 1)

            def norm(o_var, i_sq, o_inv, i_std, o_new, u, squared, summed, stded, inverted, normed, k):
                dve.wait_ge(squared, k)
                dve.tensor_reduce(o_var, i_sq, AX.X, ALU.add).then_inc(summed, 1)
                dve.wait_ge(stded, k)
                dve.reciprocal(o_inv, i_std).then_inc(inverted, 1)
                dve.wait_ge(inverted, k)
                width = u.shape[1]
                dve.tensor_tensor(o_new, u, o_inv.unsqueeze(2).to_broadcast([P, width, D]), ALU.mult).then_inc(normed, 1)

            def norm_d(h, n, k, o_new):
                norm(d_var[h][:, :], d_sq[h][:, :, :], d_inv[h][:, :], d_std[h][:, :], o_new, d_u[h][:, :, :],
                     d_sqs[h], d_vs[h], d_sd[h], d_iv[h], d_xs[h], 2 * n + k)

            def add_bias(h, a, l):
                dve.tensor_tensor(d_u[h][:, :, :], a, bias[l][0:P, :, :], ALU.add).then_inc(d_us[h], 1)

            def from_psum(b, h, k, l):
                dve.wait_ge(d_mm[h], k)
                add_bias(h, b[0:P, :].rearrange("p (r d) -> p r d", d=D), l)

            def dense_a(n):
                yield
                yield
                from_psum(d_bank[0], 0, n + 1, 0)
                yield
                norm_d(0, n, 1, d_x[0][:, :, :])
                dve.wait_ge(d_xs[0], 2 * n + 1)
                add_bias(0, d_x[0][:, :, :], 1)
                yield
                again(dve, d_tr[1], 2, n)
                norm_d(0, n, 2, d_x[1][:, :, :])

            def dense_b(n):
                yield
                from_psum(d_bank_b, 1, 2 * n + 1, 2)
                yield
                norm_d(1, n, 1, d_x[2][:, :, :])
                yield
                yield
                from_psum(d_bank_b, 1, 2 * n + 2, 3)
                yield
                again(dve, d_store, 32, n)
                norm_d(1, n, 2, d_out[:, :, :])

            def bias_rows(l, t, c):
                y = L[l]
                width = CT if l == 3 else 2 * CT
                dve.wait_ge(prod[c], y.n0 + t + 1)
                if l == 1:
                    dve.wait_ge(y.rows[c], 32 * t + 32)
                    dve.tensor_tensor(e_u[c][:, :, :], e_bank[c][0][0:P, :].rearrange("p (r d) -> p r d", d=D),
                                      e_rows[c][:, :, :].rearrange("p q (k d) -> p (q k) d", k=2), ALU.add).then_inc(biased[c], 1)
                    return
                if l == 2:
                    dve.tensor_tensor(e_u[c][:, :, :], e_bank[c][0][0:P, :].rearrange("p (r d) -> p r d", d=D),
                                      e_u[c][:, :, :], ALU.add).then_inc(biased[c], 1)
                    return
                dve.tensor_tensor(e_u[c][:, 0:width, :], e_bank[c][0][0:P, 0:width * D].rearrange("p (r d) -> p r d", d=D),
                                  bias[l][0:P, 0:width, :], ALU.add).then_inc(biased[c], 1)

            def tail(l, t, c):
                y = L[l]
                width = CT if l == 3 else 2 * CT
                again(dve, y.stored[c], 16 * CT if l == 3 else 32, t)
                norm(e_var[c][:, 0:width], e_sq[c][:, 0:width, :], e_inv[c][:, 0:width], e_std[c][:, 0:width],
                     e_new[c][:, 0:width, :], e_u[c][:, 0:width, :], sq[c], summed[c], std[c], inv[c], new[c], y.n0 + t + 1)

            def scan(l, t, c, o, i, before, rows, op0, op1, last):
                y = L[l]
                dve.wait_ge(y.flag[c], 16 * t + 16)
                if c == 1:
                    dve.wait_ge(scanned[0], y.n0 + t + 1)
                else:
                    again(dve, scanned[1], 1, y.n0 + t)
                ins = dve.tensor_tensor_scan(o[0:rows, :], e_mask[c][0:rows, :], i, before[0:rows, CE - 1:CE], op0, op1)
                if last:
                    ins.then_inc(scanned[c], 1)

            def layer0(t, c):
                dve.wait_ge(tr[c], L[0].n0 + t + 1)
                dve.tensor_copy(e_srcT[c][0:DE, :], e_bank[c][1][0:DE, 0:CE]).then_inc(attr_T[c], 1)
                yield
                yield
                dve.wait_ge(msg_sb[c], t + 1)
                scan(0, t, c, e_agg[c], e_msg[c][:, :], e_agg[1 - c], D, ALU.mult, ALU.add, True)
                yield
                yield
                bias_rows(0, t, c)
                yield
                tail(0, t, c)

            def layer1(t, c):
                dve.wait_ge(tr[c], L[1].n0 + t + 1)
                scan(1, t, c, e_agg[c], e_bank[c][1][0:D, 0:CE], e_agg[1 - c], D, ALU.mult, ALU.add, True)
                yield
                bias_rows(1, t, c)
                yield
                tail(1, t, c)

            def layer2(t, c):
                dve.wait_ge(tr[c], L[2].n0 + t + 1)
                scan(2, t, c, e_deg[c], ones_row[:, :], e_deg[1 - c], 1, ALU.mult, ALU.add, False)
                scan(2, t, c, e_agg[c], e_bank[c][1][:, 0:CE], e_agg[1 - c], D2, ALU.mult, ALU.add, True)
                yield
                m = e_small[c]
                step = stepper(dve, stat[c], STAT_STEPS, t)
                step(dve.tensor_reduce(m[:, 8, :], e_rows[c][:, :, 0:D], AX.X, ALU.add))
                dve.wait_ge(own_sq[c], t + 1)
                step(dve.tensor_reduce(m[:, 9, :], e_u[c][:, 0:CT, :], AX.X, ALU.add))
                dve.wait_ge(sums[c], t + 1)
                got = e_bank[c][1][0:P, 0:2 * CT].rearrange("p (q k) -> p q k", k=2)
                step(dve.tensor_tensor(m[:, 2, :], got[:, :, 0], m[:, 8, :], ALU.add))
                step(dve.tensor_tensor(m[:, 3, :], got[:, :, 1], m[:, 9, :], ALU.add))
                step(dve.tensor_scalar(m[:, 0, :], e_bank[c][1][0:P, 2 * CT:3 * CT], float(D), float(D), ALU.mult, ALU.add))
                step(dve.reciprocal(m[:, 1, :], m[:, 0, :]))
                step(dve.tensor_tensor(m[:, 4, :], m[:, 2, :], m[:, 1, :], ALU.mult))
                step(dve.tensor_copy(e_mean2[c][:, :, 0], m[:, 4, :]))
                step(dve.tensor_tensor(m[:, 5, :], m[:, 0, :], m[:, 4, :], ALU.mult))
                step(dve.tensor_tensor(m[:, 5, :], m[:, 5, :], m[:, 4, :], ALU.mult))
                step(dve.tensor_tensor(m[:, 6, :], m[:, 3, :], m[:, 5, :], ALU.subtract))
                step(dve.tensor_scalar(m[:, 7, :], m[:, 0, :], -1.0, None, ALU.add))
                step(dve.reciprocal(m[:, 7, :], m[:, 7, :]))
                step(dve.tensor_tensor(m[:, 6, :], m[:, 6, :], m[:, 7, :], ALU.mult))
                dve.tensor_scalar(m[:, 6, :], m[:, 6, :], 0.0, None, ALU.max).then_inc(var_ok[c], 1)
                yield
                dve.wait_ge(raw_std[c], t + 1)
                step(dve.tensor_scalar(m[:, 10, :], m[:, 10, :], EPS, None, ALU.add))
                step(dve.reciprocal(e_rstd2[c][:, :, 0], m[:, 10, :]))
                rows = e_rows[c][:, :, :].rearrange("p q (k d) -> p (q k) d", k=2)
                wide = lambda a: a[:, :, :].rearrange("p q k -> p (q k)").unsqueeze(2).to_broadcast([P, 2 * CT, D])
                step(dve.tensor_tensor(e_u[c][:, :, :], rows, bias[2][0:P, :, :], ALU.add))
                step(dve.tensor_tensor(e_sq[c][:, :, :], rows, wide(e_mean2[c]), ALU.subtract))
                dve.tensor_tensor(e_sq[c][:, :, :], e_sq[c][:, :, :], wide(e_rstd2[c]), ALU.mult).then_inc(scaled[c], 1)
                yield
                yield
                bias_rows(2, t, c)
                yield
                tail(2, t, c)

            def layer3(t, c):
                dve.wait_ge(tr[c], L[3].n0 + t + 1)
                dve.tensor_copy(e_srcT[c][0:D, :], e_bank[c][1][0:D, 0:CE]).then_inc(srcT3[c], 1)
                yield
                dve.wait_ge(vz[c], t + 1)
                scan(3, t, c, e_agg[c], e_bank[c][1][0:D, 0:CE], e_agg[1 - c], D, ALU.add, ALU.max, True)
                dve.wait_ge(scanned[c], L[3].n0 + t + 1)
                dve.tensor_tensor(e_msg[c][:, :], e_bank[c][0][0:D, 0:CE], e_agg[c][0:D, :], ALU.add).then_inc(z_in[c], 1)
                yield
                bias_rows(3, t, c)
                yield
                tail(3, t, c)

            def know_sources(t):
                for c in range(2):
                    dve.wait_ge(slot_got[c], 16 * CT * t + 16 * CT)
                    step = stepper(dve, slot_fix[c], 2, t)
                    step(dve.tensor_scalar(e_fix[c][:, :], tile_cols(edge2, t, c), 2.0, None, ALU.add))
                    step(dve.scalar_tensor_tensor(e_fix[c][:, :], e_slot[c][:, :], 0.0, e_fix[c][:, :], ALU.is_lt, ALU.mult))
                    dve.tensor_tensor(tile_cols(source_row, t, c), e_slot[c][:, :], e_fix[c][:, :], ALU.add).then_inc(src_known[c], 1)

            phases(dve, (dense_a, dense_b), (layer0, layer1, layer2, layer3), know_sources)


_INS = ['x', 'src', 'dst', 'edge_attr_32', 'L0_gnn_mW1', 'L0_gnn_mb1', 'L0_gnn_mW2', 'L0_gnn_mb2', 'L0_gnn_uW1',
        'L0_gnn_ub1', 'L0_gnn_uW2', 'L0_gnn_ub2', 'L1_gnn_W', 'L1_gnn_b', 'L2_gnn_gamma', 'L2_gnn_beta',
        'L3_gnn_W_edge', 'L3_gnn_b_edge', 'L3_gnn_W_res', 'L3_gnn_b_res']


def kernel(**inputs):
    import numpy as _np
    import concourse.bacc as _bacc
    from concourse import mybir as _mybir
    from concourse.bass_utils import run_bass_kernel_spmd as _run

    nc = _bacc.Bacc("TRN2", target_bir_lowering=False, num_devices=1)
    arrays, args = {}, []
    for name in _INS:
        a = _np.ascontiguousarray(inputs[name])
        arrays[f"in_{name}_dram"] = a
        args.append(nc.dram_tensor(f"in_{name}_dram", a.shape, _mybir.dt.from_np(a.dtype), kind="ExternalInput").ap())
    args.append(nc.dram_tensor("out_dram", inputs['x'].shape, _mybir.dt.float32, kind="ExternalOutput").ap())
    build_gnn(nc, *args)
    r = _run(nc, [arrays], core_ids=[0])
    return r.results[0]["out_dram"]
```

```python
def build_gnn(nc, x, src, dst, edge_attr, mW1, mb1, mW2, mb2, uW1, ub1, uW2, ub2,
              W1, b1, gamma, beta, W_edge, b_edge, W_res, b_res, out):
    import concourse.bass as bass
    from concourse import mybir
    from contextlib import ExitStack

    f32 = mybir.dt.float32
    i32 = mybir.dt.int32
    ALU = mybir.AluOpType
    ACT = mybir.ActivationFunctionType
    AX = mybir.AxisListType

    N, D = x.shape
    E, DE = edge_attr.shape
    HID = mW1.shape[1]
    P = 125
    D2 = 2 * D
    CT = 4
    CE = CT * P
    NT = E // P
    STEPS = E // (2 * CE)
    R = 8
    BLOCKS = N // (P * R)
    HALF = NT // 2
    PA = 112
    EPS = 1e-5
    STD_EPS_INV = 1.0 / EPS
    FAR = 1048576.0
    N_WORKED = 12
    N_PLAIN = 11
    STAT_STEPS = (6, 7)
    LOW = -3.0e38
    assert BLOCKS == 4 * STEPS and NT == 2 * HALF and D2 == 128 and HID == 128

    tables = [nc.dram_tensor(f"edge_rows_{l}", (E, D2), f32, kind="Internal").ap() for l in range(3)]
    src_sorted = nc.dram_tensor("src_sorted", (E, 1), i32, kind="Internal").ap()
    dst_sorted = nc.dram_tensor("dst_sorted", (E, 1), i32, kind="Internal").ap()
    attr_sorted = nc.dram_tensor("attr_sorted", (E, DE), f32, kind="Internal").ap()
    slot_table = nc.dram_tensor("slot_table", (N, 1), f32, kind="Internal").ap()
    same_row = nc.dram_tensor("same_row", (1, E), f32, kind="Internal").ap()
    forget_row = nc.dram_tensor("forget_row", (1, E), f32, kind="Internal").ap()
    gather_view = [t.rearrange("e (k d) -> (e k) d", k=2) for t in tables]

    ctx = ExitStack()
    with ctx:
        def sb(name, shape, dt=f32):
            return ctx.enter_context(nc.sbuf_tensor(name, shape, dt))

        def sem(name):
            return ctx.enter_context(nc.semaphore(name))

        ident = sb("ident", [128, 128])
        ones_row = sb("ones_row", [1, CE])
        ones_col = sb("ones_col", [128, 1])
        ones2 = sb("ones2", [128, 2])
        center2 = sb("center2", [128, 128])
        w_upd_top = sb("w_upd_top", [128, 128])
        w_upd_bot = sb("w_upd_bot", [128, 128])
        w_upd_agg = sb("w_upd_agg", [128, 128])
        w_out_a = sb("w_out_a", [128, 128])
        w_out_b = sb("w_out_b", [128, 128])
        w_msg_x = sb("w_msg_x", [128, 128])
        w_msg_e = sb("w_msg_e", [128, 128])
        w_msg_2 = sb("w_msg_2", [128, D])
        w_l1 = sb("w_l1", [128, 128])
        w_gamma = sb("w_gamma", [128, 128])
        w_l2_dense = sb("w_l2_dense", [128, 128])
        w_l3 = sb("w_l3", [128, 128])
        w_xi = sb("w_xi", [128, D])
        w_xj = sb("w_xj", [128, D])
        w_raw = sb("w_raw", [128, 4, D])
        row_mean = sb("row_mean", [128, 8])
        bias = [sb(f"bias_{l}", [128, 8, D]) for l in range(4)]
        bias_raw = sb("bias_raw", [128, 4, D])
        col_mb1 = sb("col_mb1", [128, 1])
        col_ub1 = sb("col_ub1", [128, 1])
        col_mb2 = sb("col_mb2", [D, 1])
        col_be = sb("col_be", [D, 1])
        col_gamma = sb("col_gamma", [128, 1])
        col_eps = sb("col_eps", [128, 1])
        minus_one = sb("minus_one", [P, N // P])

        dst_i = sb("dst_i", [HALF, 2, P], i32)
        src_i = sb("src_i", [HALF, 2, P], i32)
        prev_i = sb("prev_i", [HALF, 2, P], i32)
        next_i = sb("next_i", [HALF, 2, P], i32)
        dst_f = sb("dst_f", [HALF, 2, P])
        src_f = sb("src_f", [HALF, 2, P])
        near_f = sb("near_f", [HALF, 2, P])
        last_f = sb("last_f", [HALF, 2, P])
        same_f = sb("same_f", [HALF, 2, P])
        forget_f = sb("forget_f", [HALF, 2, P])
        index_cols = sb("index_cols", [P, 3, NT], i32)
        src_col, last_col = index_cols[:, 1, :], index_cols[:, 2, :]
        source_row = sb("source_row", [P, NT], i32)
        edge2_i = sb("edge2_i", [P, NT], i32)
        edge2 = sb("edge2", [P, NT])
        slot_all = sb("slot_all", [P, NT])
        slot_fill = sb("slot_fill", [P, NT])
        inv_n = sb("inv_n", [P, NT])
        inv_n1 = sb("inv_n1", [P, NT])

        disorder = sb("disorder", [HALF, 2, P])
        disorder_sum = sb("disorder_sum", [HALF, 1])
        disorder_i = sb("disorder_i", [1, 1], i32)
        SW = E // 20
        sort_i = sb("sort_i", [P, SW], i32)
        sort_dst = sb("sort_dst", [P, SW])
        sort_pos = sb("sort_pos", [P, SW])
        sort_cmp = sb("sort_cmp", [P, SW])
        sort_key = sb("sort_key", [P, 2, NT], i32)
        sort_keyf = sb("sort_keyf", [P, NT])
        sort_self = sb("sort_self", [P, NT])
        sort_own = sb("sort_own", [P, 1])
        sort_left = sb("sort_left", [P, 1])
        sort_rank = sb("sort_rank", [P, NT])
        sort_count = sb("sort_count", [P, 2048])
        sort_idx = sb("sort_idx", [P, 1], i32)
        sort_val = sb("sort_val", [P, 2], i32)
        sort_attr = sb("sort_attr", [P, DE])

        d_rows = sb("d_rows", [P, R * D])
        d_rowsT = [sb(f"d_rowsT{l}", [128, CE]) for l in range(4)]
        d_hid = [sb(f"d_hid{h}", [128, CE]) for h in range(2)]
        d_u = [sb(f"d_u{l}", [P, R, D]) for l in range(4)]
        d_sq = [sb(f"d_sq{l}", [P, R, D]) for l in range(4)]
        d_x = [sb(f"d_x{l}", [P, R, D]) for l in range(4)]
        d_var = [sb(f"d_var{l}", [P, R]) for l in range(4)]
        d_std = [sb(f"d_std{l}", [P, R]) for l in range(4)]
        d_inv = [sb(f"d_inv{l}", [P, R]) for l in range(4)]

        def two(name, shape, dt=f32):
            return [sb(f"{name}{c}", shape, dt) for c in range(2)]

        e_idx = two("e_idx", [P, 3 * CT], i32)
        e_val = two("e_val", [P, CT])
        e_slot = two("e_slot", [P, CT])
        e_rows = two("e_rows", [P, CT, D2])
        e_src = two("e_src", [P, CT, D2])
        e_attr = two("e_attr", [P, CT, DE])
        e_mask = two("e_mask", [128, CE])
        e_rowsT = two("e_rowsT", [128, CE])
        e_srcT = two("e_srcT", [128, CE])
        e_hid = two("e_hid", [128, CE])
        e_hidS = two("e_hidS", [128, CE])
        e_msg = two("e_msg", [D, CE])
        e_agg = two("e_agg", [128, CE])
        e_deg = two("e_deg", [1, CE])
        e_u = two("e_u", [P, 2 * CT, D])
        e_sq = two("e_sq", [P, 2 * CT, D])
        e_own = two("e_own", [P, CT, D])
        e_new = two("e_new", [P, 2 * CT, D])
        e_var = two("e_var", [P, 2 * CT])
        e_std = two("e_std", [P, 2 * CT])
        e_inv = two("e_inv", [P, 2 * CT])
        e_stat = sb("e_stat", [P, 8, 2, CT])

        bank = [ctx.enter_context(nc.psum_tensor(f"bank{i}", [128, 512], f32)) for i in range(8)]
        d_bank = bank[0:4]
        e_bank = [bank[4:6], bank[6:8]]

        k_zero = sem("k_zero")
        k_ident = sem("k_ident")
        ld_w = sem("ld_w")
        ld_p = sem("ld_p")
        ld_i = sem("ld_i")
        ld_o = sem("ld_o")
        copied = sem("copied")
        falls = sem("falls")
        falls_sum = sem("falls_sum")
        order_known = sem("order_known")
        in_order = sem("in_order")
        sort_in = sem("sort_in")
        sort_out = sem("sort_out")
        k_dve = sem("k_dve")
        k_flags = sem("k_flags")
        k_tr = sem("k_tr")
        k_idx = sem("k_idx")
        k_ready = sem("k_ready")
        flags_out = sem("flags_out")
        slots_clear = sem("slots_clear")

        def pair(name):
            return [sem(f"{name}_{c}") for c in range(2)]

        slots_set = pair("slots_set")
        slot_idx = pair("slot_idx")
        slot_got = pair("slot_got")
        slot_kept = pair("slot_kept")
        src_known = sem("src_known")
        count_flag = pair("count_flag")
        count_scan = pair("count_scan")
        count_col = pair("count_col")
        count_kept = pair("count_kept")

        d_load, d_hm, d_relu, d_store = [
            sem(f"dense_{n}") for n in ("loaded", "hidden", "relu", "stored")]
        d_tr, d_ev, d_mm, d_us, d_sqs, d_vs, d_sd, d_iv, d_xs = [
            [sem(f"dense_{n}{l}") if l != 1 or n not in ("transposed", "evacuated", "product") else None for l in range(4)]
            for n in ("transposed", "evacuated", "product", "biased", "squared", "summed", "std", "inverse", "normed")]

        class Layer:
            pass

        L = [Layer() for _ in range(4)]
        idx = pair("idx")
        flag = pair("flag")
        own_rows = pair("own_rows")
        tr = pair("tr")
        scanned = pair("scanned")
        rowsT = pair("rowsT")
        prod = pair("prod")
        biased = pair("biased")
        sq = pair("sq")
        summed = pair("summed")
        std = pair("std")
        inv = pair("inv")
        new = pair("new")
        for l, y in enumerate(L):
            y.n0 = l * STEPS
            y.r0 = STEPS if l == 3 else 0
            y.s0 = (l - 1) * STEPS
        got_x = pair("got_x")
        got = pair("got")
        stored = pair("stored")
        scattered = pair("scattered")
        attr = pair("attr")
        attr_T = pair("attr_T")
        msg_hid = pair("msg_hid"); msg_relu = pair("msg_relu")
        msg_out = pair("msg_out"); msg_sb = pair("msg_sb")
        upd_hid = pair("upd_hid"); upd_relu = pair("upd_relu")
        src_sq = pair("src_sq"); own_sq = pair("own_sq")
        sums = pair("sums"); stat = pair("stat"); raw_std = sem("raw_std"); var_ok = sem("var_ok")
        scaled = pair("scaled"); scaled_tr = pair("scaled_tr"); scaled_T = pair("scaled_T")
        last_idx = pair("last_idx")
        srcT3 = pair("srcT3"); vz = pair("vz"); z_in = pair("z_in"); z_relu = pair("z_relu")

        block = ctx.enter_context(nc.Block())

        def in_turn(*chains):
            live = list(chains)
            while live:
                for chain in list(live):
                    if next(chain, "end") == "end":
                        live.remove(chain)

        base = {0: 1, "slots": STEPS + 1, 1: 2 * STEPS + 2, 2: 3 * STEPS + 3}

        order = {0: (3, 2, 1, "edges", 0), "slots": (3, 2, 1, 0, "edges"), 1: (3, 2, "edges", 1, 0),
                 2: ("edges", 3, 2, 1, 0), "alone": (3, 2, 1, 0)}

        def phases(eng, dense, layers, slots, after_slots=None):
            def dense_step(phase, n, edges=()):
                chains = []
                for k in order[phase]:
                    if k == "edges":
                        chains.extend(edges)
                    elif not isinstance(n, int) or 0 <= n - k < BLOCKS:
                        chains.append(dense[k](n - k))
                in_turn(*chains)

            def run(first, peeled, step, last=0):
                for t in range(peeled):
                    step(first, t)
                with eng.Fori(peeled, STEPS - last) as t:
                    step(first, t)
                for t in range(STEPS - last, STEPS):
                    step(first, t)

            def layer_step(l):
                def step(first, t):
                    edges = [layers[l](t, c) for c in range(2)]
                    if l < 3:
                        dense_step(l, first + t, edges)
                    else:
                        in_turn(*edges)
                return step

            def slots_step(first, t):
                dense_step("slots", first + t, [slots(t, 0), slots(t, 1)])

            dense_step("alone", 0)
            run(base[0], 3, layer_step(0))
            run(base["slots"], 1, slots_step)
            if after_slots is not None:
                after_slots()
            dense_step("alone", base[1] - 1)
            run(base[1], 1, layer_step(1))
            dense_step("alone", base[2] - 1)
            run(base[2], 1, layer_step(2), last=3)
            run(0, 1, layer_step(3))

        def again(eng, s, per, t):
            if not isinstance(t, int) or t > 0:
                eng.wait_ge(s, per * t)

        def stepper(eng, s, per, t):
            done = [0]

            def step(ins):
                done[0] += 1
                ins.then_inc(s, 1)
                eng.wait_ge(s, per * t + done[0])
            return step

        def rows_dma(eng, o, i, s):
            eng.dma_start(o[0:PA], i[0:PA]).then_inc(s, 16)
            eng.dma_start(o[PA:P], i[PA:P]).then_inc(s, 16)

        def dense_rows(a, n):
            return a[bass.ds(n * (P * R), P * R), :].rearrange("(p r) d -> p r d", r=R)

        def edge_cols(a, t, c):
            return a[0:1, bass.ds(t * (2 * CE) + c * CE, CE)]

        def edge_rows(a, t, c):
            return a[bass.ds(t * (2 * CE) + c * CE, CE), :].rearrange("(j p) d -> p j d", p=P)

        def tile_cols(a, t, c):
            return a[:, bass.ds(t * (2 * CT) + c * CT, CT)]

        def step_cols(a, t):
            return a[:, bass.ds(t * (2 * CT), 2 * CT)].rearrange("p (c q) -> p c q", c=2)

        @block.sync
        def _(sp):
            def halves(a, lo):
                return a[lo:lo + 2 * HALF * P].rearrange("(g t p) -> t g p", g=2, p=P)

            sp.wait_ge(k_zero, 1)

            def load_dst(d, s):
                sp.dma_start(dst_i[:, :, :], halves(d, 0)).then_inc(s, 16)
                sp.dma_start(prev_i[0:1, 0, 1:P], d[0:P - 1].rearrange("(a p) -> a p", a=1)).then_inc(s, 16)
                sp.dma_start(prev_i[1:HALF, 0, :], d[P - 1:HALF * P - 1].rearrange("(t p) -> t p", p=P)).then_inc(s, 16)
                sp.dma_start(prev_i[:, 1, :], d[HALF * P - 1:E - 1].rearrange("(t p) -> t p", p=P)).then_inc(s, 16)

            load_dst(dst, ld_o)
            for o, i in ((dst_sorted, dst), (src_sorted, src)):
                sp.dma_start(o[:, 0].rearrange("(k m) -> k m", k=8), i.rearrange("(k m) -> k m", k=8)).then_inc(copied, 16)
            sp.dma_start(attr_sorted.rearrange("(k m) d -> k (m d)", k=200), edge_attr.rearrange("(k m) d -> k (m d)", k=200)).then_inc(copied, 16)
            sp.wait_ge(k_zero, 2)
            col = lambda a: a.rearrange("(p o) -> p o", o=1)
            for n, (o, i) in enumerate((
                (w_raw[:, 0, :], uW2), (w_raw[0:D, 1, :], W1),
                (w_raw[0:D, 2, :], W_res), (w_raw[D:D2, 2, :], W_res),
                (w_xi[0:D, :], W_edge[0:D, :]), (w_xj[0:D, :], W_edge[D:D2, :]),
                (col_gamma[0:D, :], col(gamma)), (col_gamma[D:D2, :], col(gamma)),
                (bias_raw[:, 0, :], ub2.partition_broadcast(128)), (bias_raw[:, 1, :], b1.partition_broadcast(128)),
                (bias_raw[:, 2, :], beta.partition_broadcast(128)), (bias_raw[:, 3, :], b_res.partition_broadcast(128)),
                (w_upd_top[0:D, :], uW1[0:D, :]), (w_upd_bot[D:D2, :], uW1[0:D, :]),
                (w_upd_agg[0:D, :], uW1[D:D2, :]),
                (w_msg_x[0:D, :], mW1[D:D2, :]), (w_msg_x[D:D2, :], mW1[0:D, :]),
                (w_msg_e[0:DE, :], mW1[D2:D2 + DE, :]), (w_msg_2[:, :], mW2),
                (col_mb1[:, :], col(mb1)), (col_ub1[:, :], col(ub1)), (col_mb2[:, :], col(mb2)),
                (col_be[:, :], col(b_edge)),
            )):
                sp.dma_start(o, i).then_inc(ld_w if n < N_WORKED else ld_p, 16)
            sp.wait_ge(in_order, 1)
            dst_o, src_o = dst_sorted[:, 0], src_sorted[:, 0]
            load_dst(dst_o, ld_i)
            sp.dma_start(src_i[:, :, :], halves(src_o, 0)).then_inc(ld_i, 16)
            sp.dma_start(next_i[:, 0, :], dst_o[1:HALF * P + 1].rearrange("(t p) -> t p", p=P)).then_inc(ld_i, 16)
            sp.dma_start(next_i[0:HALF - 1, 1, :], dst_o[HALF * P + 1:E - P + 1].rearrange("(t p) -> t p", p=P)).then_inc(ld_i, 16)
            sp.dma_start(next_i[HALF - 1:HALF, 1, 0:P - 1], dst_o[E - P + 1:E].rearrange("(a p) -> a p", a=1)).then_inc(ld_i, 16)
            sp.dma_start(slot_table.rearrange("(p k) o -> p (k o)", p=P), minus_one[:, :]).then_inc(slots_clear, 16)
            sp.wait_ge(k_flags, 1)
            sp.dma_start(halves(same_row[0, :], 0), same_f[:, :, :]).then_inc(flags_out, 16)
            sp.dma_start(halves(forget_row[0, :], 0), forget_f[:, :, :]).then_inc(flags_out, 16)
            sp.wait_ge(flags_out, 32)

            def load_dense(n):
                again(sp, d_tr[0], 1, n)
                rows_dma(sp, d_rows[:, :].rearrange("p (r d) -> p r d", r=R), dense_rows(x, n), d_load)

            def store_dense(n):
                sp.wait_ge(d_xs[3], n + 1)
                rows_dma(sp, dense_rows(out, n), d_x[3], d_store)

            def load(l, t, c):
                y = L[l]
                again(sp, scanned[c], 1, y.n0 + t)
                flags = forget_row if l == 3 else same_row
                sp.dma_start(e_mask[c][:, :], edge_cols(flags, t, c)[0, :].partition_broadcast(128)).then_inc(flag[c], 16)
                if l == 0:
                    again(sp, tr[c], 1, t)
                    rows_dma(sp, e_attr[c], edge_rows(attr_sorted, t, c), attr[c])
                else:
                    if l == 1:
                        again(sp, biased[c], 1, y.n0 + t)
                    elif l == 2:
                        again(sp, scaled_tr[c], 1, t)
                    else:
                        again(sp, tr[c], 1, y.n0 + t)
                    rows_dma(sp, e_rows[c], edge_rows(tables[l - 1], t, c), own_rows[c])

            def store(l, t, c):
                y = L[l]
                sp.wait_ge(new[c], y.n0 + t + 1)
                rows = e_new[c][:, :, :].rearrange("p (j k) d -> p j (k d)", k=2)
                rows_dma(sp, edge_rows(tables[l], t, c), rows, stored[c])

            def step(l, t, loaded=False):
                n = base[l] + t
                for c in range(2):
                    load(l, t, c)
                if not loaded and (not isinstance(n, int) or n < BLOCKS):
                    load_dense(n)
                if not isinstance(t, int) or t > 0:
                    for c in range(2):
                        store(l, t - 1, c)
                if not isinstance(n, int) or n >= 4:
                    store_dense(n - 4)

            def store_last(l):
                for c in range(2):
                    store(l, STEPS - 1, c)

            def all_stored(l):
                for c in range(2):
                    sp.wait_ge(stored[c], 32 * (L[l].n0 + STEPS))

            def slots_step(t):
                for c in range(2):
                    again(sp, count_scan[c], 1, t)
                    sp.dma_start(e_mask[c][0:1, :], edge_cols(same_row, t, c)).then_inc(count_flag[c], 16)
                load_dense(base["slots"] + t)
                store_dense(base["slots"] + t - 4)

            load_dense(0)
            for t in range(3):
                step(0, t)
            with sp.Fori(3, STEPS) as t:
                step(0, t)
            store_last(0)
            slots_step(0)
            with sp.Fori(1, STEPS) as t:
                slots_step(t)
            load_dense(base[1] - 1)
            store_dense(base[1] - 5)
            all_stored(0)
            for c in range(2):
                sp.wait_ge(count_scan[c], STEPS)
            step(1, 0)
            with sp.Fori(1, STEPS) as t:
                step(1, t)
            load_dense(base[2] - 1)
            store_last(1)
            store_dense(base[2] - 5)
            load_dense(base[2])
            all_stored(1)
            step(2, 0, loaded=True)
            with sp.Fori(1, STEPS - 3) as t:
                step(2, t)
            for t in range(STEPS - 3, STEPS):
                step(2, t)
            store_dense(BLOCKS - 1)
            store_last(2)
            all_stored(2)
            for c in range(2):
                load(3, 0, c)
            with sp.Fori(1, STEPS) as t:
                for c in range(2):
                    load(3, t, c)
            sp.wait_ge(d_store, 32 * BLOCKS)
            for c in range(2):
                sp.wait_ge(slots_set[c], 16 * CT * STEPS)
                sp.wait_ge(scattered[c], 16 * CT * STEPS)
            sp.wait_ge(slots_clear, 16)

        @block.gpsimd
        def _(pool):
            pool.memset(prev_i[:, :, :], -1)
            pool.memset(next_i[:, :, :], -1).then_inc(k_zero, 1)
            pool.memset(minus_one[:, :], -1.0)
            pool.memset(ones_row[:, :], 1.0)
            pool.memset(ones2[:, :], 0.0)
            pool.memset(ones_col[:, :], 1.0)
            pool.memset(col_eps[:, :], EPS)
            for w in (w_upd_top, w_upd_bot, w_upd_agg, w_out_a, w_out_b, w_msg_e, w_l1, w_l2_dense, w_l3,
                      w_gamma, center2, w_xi, w_xj):
                pool.memset(w[:, :], 0.0)
            for c in range(2):
                pool.memset(e_agg[c][:, :], 0.0)
                pool.memset(e_srcT[c][:, :], 0.0)
                pool.memset(e_hid[c][:, :], 0.0)
                pool.memset(e_deg[c][:, :], 0.0)
            pool.memset(ident[:, :], 0.0).then_inc(k_zero, 1)
            pool.iota(edge2_i[:, :], pattern=[[2 * P, NT]], base=0, channel_multiplier=2).then_inc(k_ident, 1)
            pool.wait_ge(k_zero, 2)
            pool.affine_select(out=ident[:, :], in_=ident[:, :], compare_op=ALU.not_equal, fill=1.0, base=0,
                               pattern=[[-1, 128]], channel_multiplier=1).then_inc(k_ident, 1)

            pool.wait_ge(order_known, 1)
            pool.wait_ge(copied, 48)
            falling = pool.value_load(disorder_i[0:1, 0:1])
            with pool.If(falling > 0):
                for k, a in enumerate((dst, src)):
                    pool.dma_start(sort_key[:, k, :], a.rearrange("(p t) -> p t", p=P)).then_inc(sort_in, 16)
                pool.iota(sort_i[:, 0:NT], pattern=[[1, NT]], base=0, channel_multiplier=NT)
                pool.drain()
                pool.wait_ge(sort_in, 32)
                pool.tensor_copy(sort_keyf[:, :], sort_key[:, 0, :])
                pool.tensor_copy(sort_self[:, :], sort_i[:, 0:NT])
                pool.drain()
                pool.iota(sort_i[:, :], pattern=[[1, SW]], base=0, channel_multiplier=0)
                pool.drain()
                pool.tensor_copy(sort_pos[:, :], sort_i[:, :])
                pool.drain()
                with pool.Fori(0, NT) as t:
                    pool.memset(sort_count[:, :], 0.0)
                    pool.tensor_copy(sort_left[:, :], sort_self[:, bass.ds(t, 1)])
                    pool.tensor_copy(sort_own[:, :], sort_keyf[:, bass.ds(t, 1)])
                    with pool.Fori(0, E // SW) as b:
                        pool.dma_start(sort_i[:, :], dst[bass.ds(b * SW, SW)].partition_broadcast(P)).then_inc(sort_in, 16)
                        pool.drain()
                        pool.tensor_scalar(sort_cmp[:, :], sort_pos[:, :], sort_left[:, :], -0.5, ALU.is_lt, ALU.mult)
                        pool.wait_ge(sort_in, 16 * (E // SW) * t + 16 * b + 48)
                        pool.nop(nofuse=True)
                        pool.tensor_copy(sort_dst[:, :], sort_i[:, :])
                        pool.drain()
                        pool.tensor_tensor(sort_cmp[:, :], sort_cmp[:, :], sort_dst[:, :], ALU.add)
                        pool.tensor_scalar(sort_left[:, :], sort_left[:, :], -float(SW), None, ALU.add)
                        pool.drain()
                        pool.tensor_scalar(sort_cmp[:, :], sort_cmp[:, :], sort_own[:, :], None, ALU.is_lt)
                        pool.drain()
                        pool.tensor_tensor(sort_count[:, 0:SW], sort_count[:, 0:SW], sort_cmp[:, :], ALU.add)
                        pool.drain()
                    for k in range(10, -1, -1):
                        h = 2 ** k
                        pool.tensor_tensor(sort_count[:, 0:h], sort_count[:, 0:h], sort_count[:, h:2 * h], ALU.add)
                        pool.drain()
                    pool.tensor_copy(sort_rank[:, bass.ds(t, 1)], sort_count[:, 0:1])
                    pool.drain()
                with pool.Fori(0, NT) as t:
                    pool.tensor_copy(sort_idx[:, :], sort_rank[:, bass.ds(t, 1)])
                    for k in range(2):
                        pool.tensor_copy(sort_val[:, k:k + 1], sort_key[:, k, bass.ds(t, 1)])
                    pool.dma_start(sort_attr[:, :], edge_attr.rearrange("(p t) d -> p t d", p=P)[:, bass.ds(t, 1), :].rearrange("p o d -> p (o d)")).then_inc(sort_out, 16)
                    pool.wait_ge(sort_out, 64 * t + 16)
                    pool.nop(nofuse=True)
                    pool.drain()
                    for table, i in ((dst_sorted, sort_val[:, 0:1]), (src_sorted, sort_val[:, 1:2]), (attr_sorted, sort_attr[:, :])):
                        pool.indirect_dma_start(out=table, out_offset=bass.IndirectOffsetOnAxis(ap=sort_idx[:, 0:1], axis=0),
                                                in_=i, in_offset=None).then_inc(sort_out, 16)
                    pool.wait_ge(sort_out, 64 * t + 64)
                    pool.nop(nofuse=True)
            pool.nop(nofuse=True).then_inc(in_order, 1)
            pool.wait_ge(k_idx, 1)

            def copy_idx(c, t, s, n, table):
                pool.tensor_copy(e_idx[c][:, 0:CT], tile_cols(table, t, c)).then_inc(s, 1)
                pool.wait_ge(s, n + 1)
                pool.nop(nofuse=True)

            def gather(o, table, c, k, s):
                pool.indirect_dma_start(out=o, out_offset=None, in_=table, in_offset=bass.IndirectOffsetOnAxis(
                    ap=e_idx[c][:, k:k + 1], axis=0)).then_inc(s, 16)

            def scatter(table, i, c, k, s):
                pool.indirect_dma_start(out=table, out_offset=bass.IndirectOffsetOnAxis(
                    ap=e_idx[c][:, k:k + 1], axis=0), in_=i, in_offset=None,
                    bounds_check=N - 1, oob_is_err=False).then_inc(s, 16)

            def layer0(t):
                for c in range(2):
                    again(pool, tr[c], 1, t)
                    again(pool, slots_set[c], 16 * CT, t)
                    pool.tensor_copy(e_val[c][:, :], tile_cols(edge2, t, c))
                    pool.tensor_copy(e_idx[c][:, :].rearrange("p (k q) -> p k q", k=3),
                                     index_cols[:, :, bass.ds(t * (2 * CT) + c * CT, CT)]).then_inc(idx[c], 1)
                    pool.wait_ge(idx[c], t + 1)
                    pool.nop(nofuse=True)
                    for j in range(CT):
                        gather(e_rows[c][:, j, 0:D], x, c, j, got_x[c])
                        gather(e_rows[c][:, j, D:D2], x, c, CT + j, got_x[c])
                    for j in range(CT):
                        scatter(slot_table, e_val[c][:, j:j + 1], c, 2 * CT + j, slots_set[c])

            def slots(t):
                for c in range(2):
                    again(pool, slot_kept[c], 1, t)
                    copy_idx(c, t, slot_idx[c], t, src_col)
                    for j in range(CT):
                        gather(e_slot[c][:, j:j + 1], slot_table, c, j, slot_got[c])

            def sources(l, t):
                for c in range(2):
                    again(pool, tr[c], 1, L[l].n0 + t)
                    copy_idx(c, t, idx[c], L[l].n0 + t, source_row)
                    for j in range(CT):
                        gather(e_src[c][:, j, 0:D], gather_view[l - 1], c, j, got[c])

            def results(t):
                for c in range(2):
                    again(pool, scattered[c], 16 * CT, t)
                    pool.tensor_copy(e_idx[c][:, CT:2 * CT], tile_cols(last_col, t, c)).then_inc(last_idx[c], 1)
                    pool.wait_ge(last_idx[c], t + 1)
                    pool.wait_ge(new[c], L[3].n0 + t + 1)
                    pool.nop(nofuse=True)
                    for j in range(CT):
                        scatter(out, e_new[c][:, j, :], c, CT + j, scattered[c])

            pool.wait_ge(slots_clear, 16)
            layer0(0)
            with pool.Fori(1, STEPS) as t:
                layer0(t)
            for c in range(2):
                pool.wait_ge(slots_set[c], 16 * CT * STEPS)
            slots(0)
            with pool.Fori(1, STEPS) as t:
                slots(t)
            pool.wait_ge(src_known, 1)
            for l in (1, 2):
                for c in range(2):
                    pool.wait_ge(stored[c], 32 * l * STEPS)
                sources(l, 0)
                with pool.Fori(1, STEPS) as t:
                    sources(l, t)
            for c in range(2):
                pool.wait_ge(stored[c], 32 * 3 * STEPS)
            sources(3, 0)
            sources(3, 1)
            pool.wait_ge(d_store, 32 * BLOCKS)
            results(0)
            with pool.Fori(2, STEPS) as t:
                sources(3, t)
                results(t - 1)
            results(STEPS - 1)

        @block.tensor
        def _(pe):
            pe.wait_ge(k_zero, 2)
            pe.wait_ge(falls, 1)
            pe.matmul(bank[4][0:1, 0:1], disorder_sum[:, :], ones_col[0:HALF, :], start=True, stop=True).then_inc(falls_sum, 1)
            pe.wait_ge(k_ident, 2)
            pe.wait_ge(ld_w, 16 * N_WORKED)
            pe.transpose(bank[3][0:D, 0:D], w_raw[0:D, 1, :], ident[0:D, 0:D]).then_inc(k_tr, 1)
            pe.wait_ge(k_flags, 1)
            for k, a in enumerate((dst_f, src_f, last_f)):
                for g in range(2):
                    last = pe.transpose(bank[k][0:P, g * HALF:(g + 1) * HALF], a[:, g, :], ident[0:HALF, 0:HALF])
            last.then_inc(k_tr, 1)
            pe.wait_ge(ld_p, 16 * N_PLAIN)
            pe.wait_ge(k_ready, 1)

            def pair_transposes(o, rows, s):
                for q in range(CT):
                    last = pe.transpose(o[:, q * P:(q + 1) * P], rows(q), ident[0:P, 0:P])
                if s is not None:
                    last.then_inc(s, 1)
                return last

            def products(o, width, terms, s):
                for q in range(CT):
                    for k, (a, w) in enumerate(terms):
                        last = pe.matmul(o[0:P, q * width:(q + 1) * width], a[:, q * P:(q + 1) * P], w,
                                         start=k == 0, stop=k == len(terms) - 1)
                last.then_inc(s, 1)

            def dense0(n):
                b0, b1 = d_bank[0:2]
                pe.wait_ge(d_load, 32 * n + 32)
                again(pe, d_relu, 1, n)
                pair_transposes(b1, lambda q: d_rows[:, q * D2:(q + 1) * D2], d_tr[0])
                yield
                pe.wait_ge(d_ev[0], n + 1)
                again(pe, d_us[0], 1, n)
                pe.matmul(b0[:, 0:CE], w_upd_top[:, :], d_rowsT[0][:, :], start=True, stop=True)
                pe.matmul(b1[:, 0:CE], w_upd_bot[:, :], d_rowsT[0][:, :], start=True, stop=True).then_inc(d_hm, 1)
                yield
                pe.wait_ge(d_relu, n + 1)
                products(b0, D2, ((d_hid[0], w_out_a[:, :]), (d_hid[1], w_out_b[:, :]), (d_rowsT[0], center2[:, :])), d_mm[0])

            def dense1(n):
                yield

            def dense_linear(n, l, w):
                pe.wait_ge(d_xs[l - 1], n + 1)
                again(pe, d_us[l], 1, n)
                pair_transposes(d_bank[l], lambda q: d_x[l - 1][:, 2 * q:2 * q + 2, :].rearrange("p r d -> p (r d)"), d_tr[l])
                yield
                pe.wait_ge(d_ev[l], n + 1)
                products(d_bank[l], D2, ((d_rowsT[l], w[:, :]),), d_mm[l])

            def dense2(n):
                return dense_linear(n, 2, w_l2_dense)

            def dense3(n):
                return dense_linear(n, 3, w_l3)

            def counts(t, c):
                yield
                pe.wait_ge(count_scan[c], t + 1)
                again(pe, count_kept[c], 1, t)
                for q in range(CT):
                    last = pe.matmul(e_bank[c][1][0:P, q:q + 1], e_deg[c][0:1, q * P:(q + 1) * P],
                                     ones_row[0:1, 0:1], start=True, stop=True)
                last.then_inc(count_col[c], 1)

            def layer0(t, c):
                y, (b0, b1) = L[0], e_bank[c]
                pe.wait_ge(got_x[c], 32 * CT * t + 32 * CT)
                again(pe, biased[c], 1, y.n0 + t)
                pair_transposes(b0, lambda q: e_rows[c][:, q, :], None)
                pe.wait_ge(attr[c], 32 * t + 32)
                for q in range(CT):
                    last = pe.transpose(b1[0:DE, q * P:(q + 1) * P], e_attr[c][:, q, :], ident[0:P, 0:P])
                last.then_inc(tr[c], 1)
                yield
                pe.wait_ge(rowsT[c], y.r0 + t + 1)
                pe.wait_ge(attr_T[c], t + 1)
                pe.matmul(b0[:, 0:CE], w_msg_x[:, :], e_rowsT[c][:, :], start=True, stop=False)
                pe.matmul(b0[:, 0:CE], w_msg_e[:, :], e_srcT[c][:, :], start=False, stop=True).then_inc(msg_hid[c], 1)
                yield
                pe.wait_ge(msg_relu[c], t + 1)
                pe.matmul(b1[0:D, 0:CE], w_msg_2[:, :], e_hid[c][:, :], start=True, stop=True).then_inc(msg_out[c], 1)
                yield
                pe.wait_ge(scanned[c], y.n0 + t + 1)
                pe.matmul(b0[:, 0:CE], w_upd_top[:, :], e_rowsT[c][:, :], start=True, stop=False)
                pe.matmul(b0[:, 0:CE], w_upd_agg[:, :], e_agg[c][:, :], start=False, stop=True)
                pe.matmul(b1[:, 0:CE], w_upd_bot[:, :], e_rowsT[c][:, :], start=True, stop=True).then_inc(upd_hid[c], 1)
                yield
                pe.wait_ge(upd_relu[c], t + 1)
                products(b0, D2, ((e_hid[c], w_out_a[:, :]), (e_hidS[c], w_out_b[:, :]), (e_rowsT[c], center2[:, :])), prod[c])

            def transpose_sources(y, b1, c, t, width):
                pe.wait_ge(got[c], 16 * CT * (y.s0 + t) + 16 * CT)
                pe.nop(nofuse=True)
                for q in range(CT):
                    last = pe.transpose(b1[0:width, q * P:(q + 1) * P], e_src[c][:, q, 0:width], ident[0:P, 0:P])
                last.then_inc(tr[c], 1)

            def transpose_rows(y, b0, c, t):
                pe.wait_ge(own_rows[c], 32 * (y.n0 - STEPS + t) + 32)
                again(pe, biased[c], 1, y.n0 + t)
                pair_transposes(b0, lambda q: e_rows[c][:, q, :], None)

            def layer1(t, c):
                y, (b0, b1) = L[1], e_bank[c]
                if isinstance(t, int):
                    pe.wait_ge(count_kept[c], STEPS)
                again(pe, scanned[c], 1, y.n0 + t)
                transpose_sources(y, b1, c, t, D)
                yield
                pe.wait_ge(scanned[c], y.n0 + t + 1)
                again(pe, biased[c], 1, y.n0 + t)
                products(b0, D2, ((e_agg[c], w_l1[:, :]),), prod[c])

            def layer2(t, c):
                y, (b0, b1) = L[2], e_bank[c]
                again(pe, scaled_T[c], 1, t)
                pe.wait_ge(src_sq[c], t + 1)
                transpose_sources(y, b1, c, t, D2)
                yield
                pe.wait_ge(scanned[c], y.n0 + t + 1)
                for q in range(CT):
                    last = pe.matmul(b1[0:P, 2 * q:2 * q + 2], e_agg[c][:, q * P:(q + 1) * P], ones2[:, :], start=True, stop=True)
                last.then_inc(sums[c], 1)
                yield
                yield
                pe.wait_ge(scaled[c], t + 1)
                pair_transposes(b1, lambda q: e_rows[c][:, q, :], scaled_tr[c])
                yield
                pe.wait_ge(scaled_T[c], t + 1)
                again(pe, biased[c], 1, y.n0 + t)
                products(b0, D2, ((e_srcT[c], w_gamma[:, :]),), prod[c])

            def layer3(t, c):
                y, (b0, b1) = L[3], e_bank[c]
                transpose_rows(y, b0, c, t)
                transpose_sources(y, b1, c, t, D)
                yield
                pe.wait_ge(rowsT[c], y.r0 + t + 1)
                pe.wait_ge(srcT3[c], t + 1)
                pe.matmul(b1[0:D, 0:CE], w_xj[:, :], e_srcT[c][:, :], start=True, stop=True)
                pe.matmul(b0[0:D, 0:CE], w_xi[:, :], e_rowsT[c][:, :], start=True, stop=True).then_inc(vz[c], 1)
                yield
                pe.wait_ge(z_relu[c], t + 1)
                products(b0, D, ((e_rowsT[c], w_l3[:, 0:D]), (e_hid[c], center2[:, 0:D])), prod[c])

            phases(pe, (dense0, dense1, dense2, dense3), (layer0, layer1, layer2, layer3), counts)

        @block.scalar
        def _(act):
            act.wait_ge(k_ready, 1)

            def norm(o_sq, u, var, o_std, biased, squared, summed, stded, k):
                act.wait_ge(biased, k)
                act.activation(o_sq, u, ACT.Square).then_inc(squared, 1)
                yield
                act.wait_ge(summed, k)
                act.activation(o_std, var, ACT.Sqrt, bias=col_eps[0:P, :], scale=1.0 / D).then_inc(stded, 1)

            def dense_norm(l, n):
                return norm(d_sq[l][:, :, :], d_u[l][:, :, :], d_var[l][:, :], d_std[l][:, :],
                            d_us[l], d_sqs[l], d_vs[l], d_sd[l], n + 1)

            def evacuate(b, l, n):
                again(act, d_mm[l], 1, n)
                act.wait_ge(d_tr[l], n + 1)
                act.activation(d_rowsT[l][:, :], b[:, 0:CE], ACT.Copy).then_inc(d_ev[l], 1)

            def dense0(n):
                evacuate(d_bank[1], 0, n)
                yield
                act.wait_ge(d_hm, n + 1)
                for h in range(2):
                    last = act.activation(d_hid[h][:, :], d_bank[h][:, 0:CE], ACT.Relu, bias=col_ub1[:, :])
                last.then_inc(d_relu, 1)
                yield
                yield from dense_norm(0, n)

            def dense1(n):
                yield from dense_norm(1, n)

            def dense2(n):
                evacuate(d_bank[2], 2, n)
                yield
                yield from dense_norm(2, n)

            def dense3(n):
                evacuate(d_bank[3], 3, n)
                yield
                yield from dense_norm(3, n)

            def counts(t, c):
                yield

            def tail(l, t, c, width):
                y = L[l]
                yield from norm(e_sq[c][:, 0:width, :], e_u[c][:, 0:width, :], e_var[c][:, 0:width], e_std[c][:, 0:width],
                                biased[c], sq[c], summed[c], std[c], y.n0 + t + 1)

            def rows_T(l, t, c):
                act.wait_ge(tr[c], L[l].n0 + t + 1)
                act.activation(e_rowsT[c][:, :], e_bank[c][0][:, 0:CE], ACT.Copy).then_inc(rowsT[c], 1)

            def layer0(t, c):
                rows_T(0, t, c)
                yield
                act.wait_ge(msg_hid[c], t + 1)
                act.activation(e_hid[c][:, :], e_bank[c][0][:, 0:CE], ACT.Relu, bias=col_mb1[:, :]).then_inc(msg_relu[c], 1)
                yield
                act.wait_ge(msg_out[c], t + 1)
                act.activation(e_msg[c][:, :], e_bank[c][1][0:D, 0:CE], ACT.Identity, bias=col_mb2[:, :]).then_inc(msg_sb[c], 1)
                yield
                act.wait_ge(upd_hid[c], t + 1)
                act.activation(e_hid[c][:, :], e_bank[c][0][:, 0:CE], ACT.Relu, bias=col_ub1[:, :])
                act.activation(e_hidS[c][:, :], e_bank[c][1][:, 0:CE], ACT.Relu, bias=col_ub1[:, :]).then_inc(upd_relu[c], 1)
                yield
                yield from tail(0, t, c, 2 * CT)

            def layer1(t, c):
                yield
                yield from tail(1, t, c, 2 * CT)

            def layer2(t, c):
                act.wait_ge(got[c], 16 * CT * (L[2].s0 + t) + 16 * CT)
                act.activation(e_src[c][:, :, D:D2], e_src[c][:, :, 0:D], ACT.Square).then_inc(src_sq[c], 1)
                act.wait_ge(own_rows[c], 32 * (L[2].n0 - STEPS + t) + 32)
                act.activation(e_own[c][:, :, :], e_rows[c][:, :, 0:D], ACT.Square).then_inc(own_sq[c], 1)
                yield
                if c == 1:
                    act.wait_ge(var_ok, t + 1)
                    act.activation(e_stat[:, 7, :, :], e_stat[:, 6, :, :], ACT.Sqrt).then_inc(raw_std, 1)
                yield
                yield
                act.wait_ge(scaled_tr[c], t + 1)
                act.activation(e_srcT[c][:, :], e_bank[c][1][:, 0:CE], ACT.Copy).then_inc(scaled_T[c], 1)
                yield
                yield from tail(2, t, c, 2 * CT)

            def layer3(t, c):
                rows_T(3, t, c)
                yield
                act.wait_ge(z_in[c], t + 1)
                act.activation(e_hid[c][0:D, :], e_msg[c][:, :], ACT.Relu, bias=col_be[:, :]).then_inc(z_relu[c], 1)
                yield
                yield from tail(3, t, c, CT)

            phases(act, (dense0, dense1, dense2, dense3), (layer0, layer1, layer2, layer3), counts)

        @block.vector
        def _(dve):
            link = stepper(dve, k_dve, 0, 0)
            dve.wait_ge(ld_o, 16 * 4)
            link(dve.tensor_copy(dst_f[:, :, :], dst_i[:, :, :]))
            link(dve.tensor_copy(same_f[:, :, :], prev_i[:, :, :]))
            link(dve.tensor_tensor(disorder[:, :, :], same_f[:, :, :], dst_f[:, :, :], ALU.is_gt))
            dve.tensor_reduce(disorder_sum[:, :], disorder[:, :, :], AX.XY, ALU.add).then_inc(falls, 1)
            dve.wait_ge(falls_sum, 1)
            dve.tensor_copy(disorder_i[:, :], bank[4][0:1, 0:1]).then_inc(order_known, 1)
            dve.wait_ge(k_ident, 2)
            dve.wait_ge(ld_w, 16 * N_WORKED)

            def center(o, i, p0, p1):
                link(dve.tensor_reduce(row_mean[p0:p1, 0:1], i, AX.X, ALU.add))
                link(dve.tensor_scalar(row_mean[p0:p1, 1:2], row_mean[p0:p1, 0:1], -1.0 / D, None, ALU.mult))
                link(dve.tensor_scalar(o, i, row_mean[p0:p1, 1:2], None, ALU.add))

            center(w_out_a[:, 0:D], w_raw[:, 0, :], 0, 128)
            link(dve.tensor_copy(w_out_b[:, D:D2], w_out_a[:, 0:D]))
            link(dve.memset(ones2[0:D, 0:1], 1.0))
            link(dve.memset(ones2[D:D2, 1:2], 1.0))
            dve.wait_ge(k_tr, 1)
            center(w_l1[0:D, 0:D], bank[3][0:D, 0:D], 0, D)
            link(dve.tensor_tensor(w_xi[0:D, :], w_xi[0:D, :], w_xj[0:D, :], ALU.subtract))
            link(dve.tensor_scalar(row_mean[:, 2:3], col_gamma[:, :], STD_EPS_INV, 1.0, ALU.mult, ALU.add))
            for h in range(2):
                a, b = h * D, (h + 1) * D
                center(center2[a:b, a:b], ident[a:b, a:b], a, b)
                link(dve.tensor_tensor(w_raw[a:b, 3, :], w_raw[a:b, 2, :], ident[a:b, a:b], ALU.add))
                center(w_l3[a:b, a:b], w_raw[a:b, 3, :], a, b)
                link(dve.tensor_scalar(w_gamma[a:b, a:b], center2[a:b, a:b], col_gamma[a:b, :], None, ALU.mult))
                if h == 1:
                    link(dve.tensor_scalar(w_gamma[a:b, a:b], w_gamma[a:b, a:b], STD_EPS_INV, None, ALU.mult))
                link(dve.tensor_scalar(w_l2_dense[a:b, a:b], center2[a:b, a:b], row_mean[a:b, 2:3], None, ALU.mult))
            for l in range(4):
                center(bias[l][:, 0, :], bias_raw[:, l, :], 0, 128)
                link(dve.tensor_copy(bias[l][:, 1:8, :], bias[l][:, 0:1, :].to_broadcast([128, 7, D])))
            for h in range(2):
                link(dve.tensor_copy(w_l1[D:D + 1, h * D:(h + 1) * D], bias[1][D:D + 1, 0, :]))
                link(dve.memset(e_agg[h][D:D + 1, :], 1.0))
            dve.wait_ge(ld_i, 16 * 8)
            for o, i in ((dst_f, dst_i), (src_f, src_i), (same_f, prev_i), (near_f, next_i)):
                link(dve.tensor_copy(o[:, :, :], i[:, :, :]))
            link(dve.tensor_copy(edge2[:, :], edge2_i[:, :]))
            link(dve.tensor_tensor(same_f[:, :, :], same_f[:, :, :], dst_f[:, :, :], ALU.is_equal))
            link(dve.tensor_tensor(near_f[:, :, :], near_f[:, :, :], dst_f[:, :, :], ALU.is_equal))
            link(dve.tensor_scalar(forget_f[:, :, :], same_f[:, :, :], -LOW, LOW, ALU.mult, ALU.add))
            dve.scalar_tensor_tensor(last_f[:, :, :], near_f[:, :, :], FAR, dst_f[:, :, :], ALU.mult, ALU.add).then_inc(k_flags, 1)
            dve.wait_ge(k_tr, 2)
            for k in range(3):
                link(dve.tensor_copy(index_cols[:, k, :], bank[k][0:P, 0:NT]))
            dve.engine_nop().then_inc(k_idx, 1)
            dve.engine_nop().then_inc(k_ready, 1)

            def norm(o_var, i_sq, o_inv, i_std, o_new, u, squared, summed, stded, inverted, normed, k):
                dve.wait_ge(squared, k)
                dve.tensor_reduce(o_var, i_sq, AX.X, ALU.add).then_inc(summed, 1)
                yield
                dve.wait_ge(stded, k)
                dve.reciprocal(o_inv, i_std).then_inc(inverted, 1)
                dve.wait_ge(inverted, k)
                width = u.shape[1]
                dve.tensor_tensor(o_new, u, o_inv.unsqueeze(2).to_broadcast([P, width, D]), ALU.mult).then_inc(normed, 1)

            def dense_norm(l, n):
                return norm(d_var[l][:, :], d_sq[l][:, :, :], d_inv[l][:, :], d_std[l][:, :], d_x[l][:, :, :], d_u[l][:, :, :],
                     d_sqs[l], d_vs[l], d_sd[l], d_iv[l], d_xs[l], n + 1)

            def from_psum(b, l, n):
                dve.wait_ge(d_mm[l], n + 1)
                again(dve, d_xs[l], 1, n)
                dve.tensor_tensor(d_u[l][:, :, :], b[0:P, :].rearrange("p (r d) -> p r d", d=D),
                                  bias[l][0:P, :, :], ALU.add).then_inc(d_us[l], 1)

            def dense0(n):
                yield
                yield
                from_psum(d_bank[0], 0, n)
                yield
                again(dve, d_us[1], 1, n)
                yield from dense_norm(0, n)

            def dense1(n):
                dve.wait_ge(d_xs[0], n + 1)
                again(dve, d_xs[1], 1, n)
                dve.tensor_tensor(d_u[1][:, :, :], d_x[0][:, :, :], bias[1][0:P, :, :], ALU.add).then_inc(d_us[1], 1)
                yield
                again(dve, d_tr[2], 1, n)
                yield from dense_norm(1, n)

            def dense2(n):
                yield
                from_psum(d_bank[2], 2, n)
                yield
                again(dve, d_tr[3], 1, n)
                yield from dense_norm(2, n)

            def dense3(n):
                yield
                from_psum(d_bank[3], 3, n)
                yield
                again(dve, d_store, 32, n)
                yield from dense_norm(3, n)

            def bias_rows(l, t, c):
                y = L[l]
                width = CT if l == 3 else 2 * CT
                dve.wait_ge(prod[c], y.n0 + t + 1)
                if l == 1:
                    dve.wait_ge(own_rows[c], 32 * (y.n0 - STEPS + t) + 32)
                    dve.tensor_tensor(e_u[c][:, :, :], e_bank[c][0][0:P, :].rearrange("p (r d) -> p r d", d=D),
                                      e_rows[c][:, :, :].rearrange("p q (k d) -> p (q k) d", k=2), ALU.add).then_inc(biased[c], 1)
                    return
                if l == 2:
                    dve.tensor_tensor(e_u[c][:, :, :], e_bank[c][0][0:P, :].rearrange("p (r d) -> p r d", d=D),
                                      e_u[c][:, :, :], ALU.add).then_inc(biased[c], 1)
                    return
                dve.tensor_tensor(e_u[c][:, 0:width, :], e_bank[c][0][0:P, 0:width * D].rearrange("p (r d) -> p r d", d=D),
                                  bias[l][0:P, 0:width, :], ALU.add).then_inc(biased[c], 1)

            def tail(l, t, c):
                y = L[l]
                width = CT if l == 3 else 2 * CT
                if l == 3:
                    again(dve, scattered[c], 16 * CT, t)
                else:
                    again(dve, stored[c], 32, y.n0 + t)
                yield from norm(e_var[c][:, 0:width], e_sq[c][:, 0:width, :], e_inv[c][:, 0:width], e_std[c][:, 0:width],
                     e_new[c][:, 0:width, :], e_u[c][:, 0:width, :], sq[c], summed[c], std[c], inv[c], new[c], y.n0 + t + 1)

            def scan(l, t, c, o, i, before, rows, op0, op1):
                y = L[l]
                dve.wait_ge(flag[c], 16 * (y.n0 + t) + 16)
                if c == 1:
                    dve.wait_ge(scanned[0], y.n0 + t + 1)
                else:
                    again(dve, scanned[1], 1, y.n0 + t)
                dve.tensor_tensor_scan(o[0:rows, :], e_mask[c][0:rows, :], i, before[0:rows, CE - 1:CE],
                                       op0, op1).then_inc(scanned[c], 1)

            def layer0(t, c):
                dve.wait_ge(tr[c], L[0].n0 + t + 1)
                dve.tensor_copy(e_srcT[c][0:DE, :], e_bank[c][1][0:DE, 0:CE]).then_inc(attr_T[c], 1)
                yield
                yield
                dve.wait_ge(msg_sb[c], t + 1)
                scan(0, t, c, e_agg[c], e_msg[c][:, :], e_agg[1 - c], D, ALU.mult, ALU.add)
                yield
                yield
                bias_rows(0, t, c)
                yield
                yield from tail(0, t, c)

            def layer1(t, c):
                dve.wait_ge(tr[c], L[1].n0 + t + 1)
                scan(1, t, c, e_agg[c], e_bank[c][1][0:D, 0:CE], e_agg[1 - c], D, ALU.mult, ALU.add)
                yield
                bias_rows(1, t, c)
                yield
                yield from tail(1, t, c)

            def layer2(t, c):
                dve.wait_ge(tr[c], L[2].n0 + t + 1)
                scan(2, t, c, e_agg[c], e_bank[c][1][:, 0:CE], e_agg[1 - c], D2, ALU.mult, ALU.add)
                yield
                own, own2, s1, s2, mean, prod1, var, dev = [e_stat[:, k, :, :] for k in range(8)]
                step = stepper(dve, stat[c], STAT_STEPS[c], t)
                dve.wait_ge(own_rows[c], 32 * (L[2].n0 - STEPS + t) + 32)
                step(dve.tensor_reduce(own[:, c, :], e_rows[c][:, :, 0:D], AX.X, ALU.add))
                dve.wait_ge(own_sq[c], t + 1)
                step(dve.tensor_reduce(own2[:, c, :], e_own[c][:, :, :], AX.X, ALU.add))
                dve.wait_ge(sums[c], t + 1)
                of_sources = e_bank[c][1][0:P, 0:2 * CT].rearrange("p (q k) -> p q k", k=2)
                dve.tensor_tensor(s2[:, c, :], of_sources[:, :, 1], own2[:, c, :], ALU.add)
                step(dve.tensor_tensor(s1[:, c, :], of_sources[:, :, 0], own[:, c, :], ALU.add))
                if c == 1:
                    step(dve.tensor_tensor(mean, s1, step_cols(inv_n, t), ALU.mult))
                    step(dve.tensor_tensor(prod1, s1, mean, ALU.mult))
                    step(dve.tensor_tensor(var, s2, prod1, ALU.subtract))
                    dve.scalar_tensor_tensor(var, var, 0.0, step_cols(inv_n1, t), ALU.max, ALU.mult).then_inc(var_ok, 1)
                dve.tensor_tensor(e_u[c][:, :, :], e_rows[c][:, :, :].rearrange("p q (k d) -> p (q k) d", k=2),
                                  bias[2][0:P, :, :], ALU.add)
                yield
                wide = lambda a: a.unsqueeze(2).to_broadcast([P, CT, D])
                step(dve.tensor_tensor(e_rows[c][:, :, 0:D], e_rows[c][:, :, 0:D], wide(mean[:, c, :]), ALU.subtract))
                if c == 0:
                    dve.wait_ge(raw_std, t + 1)
                    step(dve.tensor_scalar(dev, dev, EPS, None, ALU.add))
                    step(dve.reciprocal(dev, dev))
                dve.tensor_tensor(e_rows[c][:, :, 0:D], e_rows[c][:, :, 0:D], wide(dev[:, c, :]), ALU.mult).then_inc(scaled[c], 1)
                yield
                yield
                bias_rows(2, t, c)
                yield
                yield from tail(2, t, c)

            def layer3(t, c):
                dve.wait_ge(tr[c], L[3].n0 + t + 1)
                dve.tensor_copy(e_srcT[c][0:D, :], e_bank[c][1][0:D, 0:CE]).then_inc(srcT3[c], 1)
                yield
                dve.wait_ge(vz[c], t + 1)
                scan(3, t, c, e_agg[c], e_bank[c][1][0:D, 0:CE], e_agg[1 - c], D, ALU.add, ALU.max)
                dve.wait_ge(scanned[c], L[3].n0 + t + 1)
                dve.tensor_tensor(e_msg[c][:, :], e_bank[c][0][0:D, 0:CE], e_agg[c][0:D, :], ALU.add).then_inc(z_in[c], 1)
                yield
                bias_rows(3, t, c)
                yield
                yield from tail(3, t, c)

            def counts(t, c):
                dve.wait_ge(count_flag[c], 16 * t + 16)
                if c == 1:
                    dve.wait_ge(count_scan[0], t + 1)
                else:
                    again(dve, count_scan[1], 1, t)
                again(dve, count_col[c], 1, t)
                dve.tensor_tensor_scan(e_deg[c][:, :], e_mask[c][0:1, :], ones_row[:, :], e_deg[1 - c][:, CE - 1:CE],
                                       ALU.mult, ALU.add).then_inc(count_scan[c], 1)
                yield
                dve.wait_ge(slot_got[c], 16 * CT * t + 16 * CT)
                dve.tensor_copy(tile_cols(slot_all, t, c), e_slot[c][:, :]).then_inc(slot_kept[c], 1)
                dve.wait_ge(count_col[c], t + 1)
                dve.tensor_scalar(tile_cols(inv_n, t, c), e_bank[c][1][0:P, 0:CT], float(D), float(D),
                                  ALU.mult, ALU.add).then_inc(count_kept[c], 1)

            def after_slots():
                for c in range(2):
                    dve.wait_ge(slot_kept[c], STEPS)
                    dve.wait_ge(count_kept[c], STEPS)
                link(dve.tensor_scalar(slot_fill[:, :], edge2[:, :], 2.0, None, ALU.add))
                link(dve.scalar_tensor_tensor(slot_fill[:, :], slot_all[:, :], 0.0, slot_fill[:, :], ALU.is_lt, ALU.mult))
                dve.tensor_tensor(source_row[:, :], slot_all[:, :], slot_fill[:, :], ALU.add).then_inc(src_known, 1)
                link(dve.tensor_scalar(inv_n1[:, :], inv_n[:, :], -1.0, None, ALU.add))
                link(dve.reciprocal(inv_n1[:, :], inv_n1[:, :]))
                link(dve.reciprocal(inv_n[:, :], inv_n[:, :]))

            phases(dve, (dense0, dense1, dense2, dense3), (layer0, layer1, layer2, layer3), counts, after_slots)


_INS = ['x', 'src', 'dst', 'edge_attr_32', 'L0_gnn_mW1', 'L0_gnn_mb1', 'L0_gnn_mW2', 'L0_gnn_mb2', 'L0_gnn_uW1',
        'L0_gnn_ub1', 'L0_gnn_uW2', 'L0_gnn_ub2', 'L1_gnn_W', 'L1_gnn_b', 'L2_gnn_gamma', 'L2_gnn_beta',
        'L3_gnn_W_edge', 'L3_gnn_b_edge', 'L3_gnn_W_res', 'L3_gnn_b_res']


def kernel(**inputs):
    import numpy as _np
    import concourse.bacc as _bacc
    from concourse import mybir as _mybir
    from concourse.bass_utils import run_bass_kernel_spmd as _run

    nc = _bacc.Bacc("TRN2", target_bir_lowering=False, num_devices=1)
    arrays, args = {}, []
    for name in _INS:
        a = _np.ascontiguousarray(inputs[name])
        arrays[f"in_{name}_dram"] = a
        args.append(nc.dram_tensor(f"in_{name}_dram", a.shape, _mybir.dt.from_np(a.dtype), kind="ExternalInput").ap())
    args.append(nc.dram_tensor("out_dram", inputs['x'].shape, _mybir.dt.float32, kind="ExternalOutput").ap())
    build_gnn(nc, *args)
    r = _run(nc, [arrays], core_ids=[0])
    return r.results[0]["out_dram"]
```
